# Optimizing a Trainium2 kernel written in Bass

```python
import numpy as np
import jax
import jax.numpy as jnp

def _softmax(x, axis=-1):
    return jax.nn.softmax(x, axis=axis)

def _gelu(x):
    return jax.nn.gelu(x, approximate=True)

def _silu(x):
    return jax.nn.silu(x)

def _sigmoid(x):
    return jax.nn.sigmoid(x)

def _layernorm(x, axis=-1, eps=1e-05):
    m = jnp.mean(x, axis=axis, keepdims=True)
    v = jnp.var(x, axis=axis, keepdims=True)
    return (x - m) / jnp.sqrt(v + eps)

def _scatter_add(tgt, idx, src, axis=0):
    return tgt.at[idx].add(src)

def _segment_sum(src, seg, n):
    return jax.ops.segment_sum(src, seg, n)
kernel_name = 'mk_flamingo_gated_d1_seqx_r4_ee90e2'

def setup_inputs(seed: int=0):
    np.random.seed(seed)
    _w = jnp.asarray

    def _rec_inputs():
        import jax
        import jax.numpy as jnp
        _rk = jax.random.key(seed)
        x = 7.22e-05 + 1 * jax.random.normal(jax.random.fold_in(_rk, 1), (4, 1024, 256), jnp.float32)
        _lenS = 1024 - jax.random.randint(jax.random.fold_in(_rk, 7), (4,), 0, max(1, 1024 // 4) + 1, jnp.int32)
        _lenS2 = 77 - jax.random.randint(jax.random.fold_in(_rk, 8), (4,), 0, max(1, 77 // 4) + 1, jnp.int32)
        _ctx_1024P = jax.random.normal(jax.random.fold_in(_rk, 11), (4, 16, 256), jnp.float32)
        _ctx_1024c = jax.random.dirichlet(jax.random.fold_in(_rk, 511), 0.3 * jnp.ones((16,), jnp.float32), (4, 77))
        _ctx_1024t = jnp.einsum('bsk,bkd->bsd', _ctx_1024c, _ctx_1024P)
        _ctx_1024t = _ctx_1024t * jax.lax.rsqrt(jnp.mean(jnp.square(_ctx_1024t)) + 1e-12) * 0.953939
        ctx_1024 = 4.13588e-05 + 0.999923 * (_ctx_1024t + 0.3 * jax.random.normal(jax.random.fold_in(_rk, 611), (4, 77, 256), jnp.float32))
        _validS = jnp.arange(1024)[None, :] < _lenS[:, None]
        _validS2 = jnp.arange(77)[None, :] < _lenS2[:, None]
        _causal = jnp.tril(jnp.ones((1024, 1024), dtype=bool))
        mask_BxSxS2_ff0 = jnp.where(jnp.ones((4, 1024, 77), dtype=bool), 0.0, -1000000000.0).astype(jnp.float32)
        _g = jax.random.normal(jax.random.fold_in(_rk, 9001), (2, 1), jnp.float32)
        _g = jnp.sign(_g) * jnp.maximum(jnp.abs(_g), 1.0) + (_g == 0) * 1.0
        g_xattn = _g[0]
        g_ffn = _g[1]
        return (x, ctx_1024, mask_BxSxS2_ff0, g_xattn, g_ffn)
    x, ctx_1024, mask_BxSxS2_ff0, g_xattn, g_ffn = _rec_inputs()

    def _L0_xattn_setup():
        import jax, jax.numpy as jnp
        import numpy as np
        B, S, D, H = (4, 512, 256, 256)
        key = jax.random.key(seed)
        k1, k2, k3, k4, k5, k6 = jax.random.split(key, 6)
        return {'x1': jax.random.normal(k1, (B, S, D), dtype=jnp.float32), 'x2': jax.random.normal(k2, (B, S, D), dtype=jnp.float32), 'x3': jax.random.normal(k3, (B, S, D), dtype=jnp.float32), 'mask': jnp.zeros((B, S, S), dtype=jnp.float32), 'Wq': jax.random.normal(k4, (H, D), dtype=jnp.float32) * (1.0 / np.sqrt(D)), 'Wk': jax.random.normal(k5, (H, D), dtype=jnp.float32) * (1.0 / np.sqrt(D)), 'Wv': jax.random.normal(k6, (H, D), dtype=jnp.float32) * (1.0 / np.sqrt(D))}
    _L0_xattn_all = _L0_xattn_setup()
    _L0_xattn_in = {k: v for k, v in _L0_xattn_all.items() if k in ('Wq', 'Wk', 'Wv')}
    del _L0_xattn_all

    def _L0_ffn_setup():
        import jax, jax.numpy as jnp
        import numpy as np
        TAU = 1.0
        K_ROUTE = 3
        EPS = 1e-08

        def _route_combine_weights(x_addr, U, k, tau):
            z = x_addr @ U.T
            topv, topi = jax.lax.top_k(z, k)
            w = jax.nn.softmax(topv / (tau + EPS), axis=1)
            N, L = z.shape
            rows = jnp.arange(N)[:, None]
            return jnp.zeros((N, L), z.dtype).at[rows, topi].add(w)

        def _mixture(inp, C, W):
            L = W.shape[0]
            y = jnp.zeros((inp.shape[0], W.shape[1]), inp.dtype)
            for e in range(L):
                y = y + C[:, e:e + 1] * (inp @ W[e].T)
            return y
        key = jax.random.key(seed)
        ks = jax.random.split(key, 8)
        B, T, D_in, H, D_out, L, d_addr = (8, 2048, 256, 256, 256, 12, 64)

        def unit_rows(k, L_, d_):
            U = jax.random.normal(k, (L_, d_), dtype=jnp.float32)
            U = U - U.mean(axis=1, keepdims=True)
            return U / (jnp.linalg.norm(U, axis=1, keepdims=True) + EPS)

        def norm_tape(k, shape):
            W = jax.random.normal(k, shape, dtype=jnp.float32)
            n = jnp.sqrt(jnp.sum(W * W, axis=tuple(range(1, W.ndim)), keepdims=True)) + 1e-12
            return W / n
        x = jax.random.normal(ks[0], (B, T, D_in), dtype=jnp.float32)
        P_w = jax.random.normal(ks[1], (d_addr, D_in), dtype=jnp.float32) / np.sqrt(D_in)
        U1 = unit_rows(ks[2], L, d_addr)
        U2 = unit_rows(ks[3], L, d_addr)
        U3 = unit_rows(ks[4], L, d_addr)
        W1 = norm_tape(ks[5], (L, H, D_in))
        W2 = norm_tape(ks[6], (L, D_out, H))
        b2 = norm_tape(ks[7], (L, D_out))
        return {'x': x, 'P_w': P_w, 'U1': U1, 'U2': U2, 'U3': U3, 'W1': W1, 'W2': W2, 'b2': b2}
    _L0_ffn_all = _L0_ffn_setup()
    _L0_ffn_in = {k: v for k, v in _L0_ffn_all.items() if k in ('P_w', 'U1', 'U2', 'U3', 'W1', 'W2', 'b2')}
    del _L0_ffn_all
    return {'x': x, 'ctx_1024': ctx_1024, 'mask_BxSxS2_ff0': mask_BxSxS2_ff0, 'g_xattn': g_xattn, 'g_ffn': g_ffn, 'L0_xattn_Wq': _L0_xattn_in['Wq'], 'L0_xattn_Wk': _L0_xattn_in['Wk'], 'L0_xattn_Wv': _L0_xattn_in['Wv'], 'L0_ffn_P_w': _L0_ffn_in['P_w'], 'L0_ffn_U1': _L0_ffn_in['U1'], 'L0_ffn_U2': _L0_ffn_in['U2'], 'L0_ffn_U3': _L0_ffn_in['U3'], 'L0_ffn_W1': _L0_ffn_in['W1'], 'L0_ffn_W2': _L0_ffn_in['W2'], 'L0_ffn_b2': _L0_ffn_in['b2']}

def reference(x, ctx_1024, mask_BxSxS2_ff0, g_xattn, g_ffn, L0_xattn_Wq, L0_xattn_Wk, L0_xattn_Wv, L0_ffn_P_w, L0_ffn_U1, L0_ffn_U2, L0_ffn_U3, L0_ffn_W1, L0_ffn_W2, L0_ffn_b2):
    import jax
    import jax.numpy as jnp

    def _L0_xattn_ref(x1, x2, x3, mask, Wq, Wk, Wv):
        import jax, jax.numpy as jnp
        import numpy as np
        B, S, D, H = (4, 512, 256, 256)
        q = jnp.einsum('bsd,hd->bsh', x1, Wq)
        k = jnp.einsum('bsd,hd->bsh', x2, Wk)
        v = jnp.einsum('bsd,hd->bsh', x3, Wv)
        scale = 1.0 / jnp.sqrt(jnp.float32(H))
        scores = jnp.einsum('bqh,bkh->bqk', q, k) * scale
        weights = jax.nn.softmax(scores + mask, axis=-1)
        out = jnp.einsum('bqk,bkh->bqh', weights, v)
        return out

    def _L0_ffn_ref(x, P_w, U1, U2, U3, W1, W2, b2):
        import jax, jax.numpy as jnp
        import numpy as np
        TAU = 1.0
        K_ROUTE = 3
        EPS = 1e-08

        def _route_combine_weights(x_addr, U, k, tau):
            z = x_addr @ U.T
            topv, topi = jax.lax.top_k(z, k)
            w = jax.nn.softmax(topv / (tau + EPS), axis=1)
            N, L = z.shape
            rows = jnp.arange(N)[:, None]
            return jnp.zeros((N, L), z.dtype).at[rows, topi].add(w)

        def _mixture(inp, C, W):
            L = W.shape[0]
            y = jnp.zeros((inp.shape[0], W.shape[1]), inp.dtype)
            for e in range(L):
                y = y + C[:, e:e + 1] * (inp @ W[e].T)
            return y
        B, T, D = x.shape
        xf = x.reshape(B * T, D)
        xa = xf @ P_w.T
        C1 = _route_combine_weights(xa, U1, K_ROUTE, TAU)
        C2 = _route_combine_weights(xa, U2, K_ROUTE, TAU)
        C3 = _route_combine_weights(xa, U3, K_ROUTE, TAU)
        h = jax.nn.gelu(_mixture(xf, C1, W1), approximate=False)
        y = _mixture(h, C2, W2) + C3 @ b2
        return y.reshape(B, T, -1)
    x = x + jnp.tanh(g_xattn[0]) * _L0_xattn_ref(_layernorm(x, axis=-1), ctx_1024, ctx_1024, mask_BxSxS2_ff0, L0_xattn_Wq, L0_xattn_Wk, L0_xattn_Wv)
    x = x + jnp.tanh(g_ffn[0]) * _L0_ffn_ref(_layernorm(x, axis=-1), L0_ffn_P_w, L0_ffn_U1, L0_ffn_U2, L0_ffn_U3, L0_ffn_W1, L0_ffn_W2, L0_ffn_b2)
    return x

_drawn_inputs = setup_inputs


def setup_inputs(seed=0):
    import zlib

    import numpy as np

    out = dict(_drawn_inputs(seed))
    spreads = {}
    factors = {'L0_ffn_U1': 8.0, 'L0_ffn_U2': 8.0, 'L0_ffn_W1': 8.0, 'L0_ffn_W2': 8.0}
    for name, (base, spread) in spreads.items():
        noise = np.random.default_rng([zlib.crc32(name.encode()), seed]).standard_normal(out[name].shape)
        drawn = base * np.exp(spread * noise) if base else spread * noise
        out[name] = jnp.asarray(drawn.astype(out[name].dtype))
    for name, factor in factors.items():
        out[name] = (out[name] * factor).astype(out[name].dtype)
    return out
```

```python
from contextlib import ExitStack

import concourse.bass as bass
from concourse import mybir

F32 = mybir.dt.float32
F32R = mybir.dt.float32r
ALU = mybir.AluOpType
ACT = mybir.ActivationFunctionType
AX = mybir.AxisListType

LN_EPS = 1e-5
LOWEST = -3.4028234663852886e38
PICKED = 3.4028234663852886e38


def gated_xattn_and_routed_ffn(nc, x, ctx_t, mask, g_xattn, g_ffn, wq, wk_t, wv_t, p_w, u_t, w1_t, w2_t, b2, out):
    P = 128
    B, S, D = x.shape
    SC = mask.shape[2]
    L = b2.shape[0]
    KD = D // P
    TILES = B * S // P
    TPB = S // P
    R = 3
    TOPK = 3
    ZW = L + 8 - TOPK
    PAIRS = L // 2
    RING = 4
    ADDR = p_w.shape[0]
    CHUNK = 1024
    WCH = L * D // CHUNK
    NCH = KD * WCH
    STAGES = 4
    SCALE = 1.0 / float(D) ** 0.5
    BN = nc.vector.BN_STATS_DIM
    assert D == KD * P == 256 and L % 2 == 0 and 2 * D == 512 and CHUNK % D == 0 and S % P == 0

    x_rows = x.rearrange("b (n p) d -> p (b n) d", p=P)
    out_rows = out.rearrange("b (n p) d -> p (b n) d", p=P)
    mask_rows = mask.rearrange("b (n p) s -> p (b n) s", p=P)

    with ExitStack() as ctx:
        def sb(name, shape, dt=F32):
            return ctx.enter_context(nc.sbuf_tensor(name, shape, dt))

        def ps(name, shape):
            return ctx.enter_context(nc.psum_tensor(name, shape, F32))

        def sem(name):
            return ctx.enter_context(nc.semaphore(name))

        ring = ps("ring", [P, RING, 2 * D])
        turn_ps = ps("turn_ps", [P, 2 * D])
        hturn_ps = ps("hturn_ps", [P, 2 * D])
        att_ps = ps("att_ps", [P, 2 * D])
        bias_ps = ps("bias_ps", [P, 2 * D])

        xb = sb("xb", [P, TILES, D])
        maskb = sb("maskb", [P, TILES, SC])
        ident = sb("ident", [P, P])
        minus_half = sb("minus_half", [P, 1])
        eps = sb("eps", [P, 1])
        ctxb = sb("ctxb", [P, KD, B * SC])
        wqb = sb("wqb", [P, KD, D])
        wkb = sb("wkb", [P, KD, D])
        wvb = sb("wvb", [P, KD, D])
        pwb = sb("pwb", [ADDR, D])
        utb = sb("utb", [ADDR, R * L])
        b2b = sb("b2b", [L, D])
        gates = sb("gates", [P, 2])
        tg = sb("tg", [P, 2])
        b2g = sb("b2g", [L, D])
        kt = sb("kt", [P, KD, B * SC])
        qk = sb("qk", [P, KD, B * SC])
        vb = sb("vb", [SC, B, D])
        pu_hi = sb("pu_hi", [P, KD, R * L], F32R)
        pu_lo = sb("pu_lo", [P, KD, R * L], F32R)
        wstage = [sb(f"wstage{n}", [P, CHUNK]) for n in range(STAGES)]
        w1_hi = sb("w1_hi", [P, KD, L * D], F32R)
        w1_lo = sb("w1_lo", [P, KD, L * D], F32R)
        w2_hi = sb("w2_hi", [P, KD, L * D], F32R)
        w2_lo = sb("w2_lo", [P, KD, L * D], F32R)

        stats1 = sb("stats1", [P, BN])
        mv1 = sb("mv1", [P, 2])
        var1 = sb("var1", [P, 1])
        rstd1 = sb("rstd1", [P, 1])
        xn1 = sb("xn1", [P, D])
        xn1_t = sb("xn1_t", [P, KD, P])
        scores = sb("scores", [P, SC])
        neg_max = sb("neg_max", [P, 1])
        probs = sb("probs", [P, SC])
        row_sum = sb("row_sum", [P, 1])
        inv_sum = sb("inv_sum", [P, 1])
        probs_t = sb("probs_t", [SC, P])
        stats2 = sb("stats2", [P, BN])
        mv2 = sb("mv2", [P, 2])
        var2 = sb("var2", [P, 1])
        rstd2 = sb("rstd2", [P, 1])
        xn2 = sb("xn2", [P, D])
        x2_hi = sb("x2_hi", [P, KD, P], F32R)
        x2_lo = sb("x2_lo", [P, KD, P], F32R)
        z = sb("z", [P, R, ZW])
        top = sb("top", [P, R, 8])
        wanted = sb("wanted", [P, R, 8])
        marked = sb("marked", [P, R, ZW])
        zs = sb("zs", [P, R, L])
        ez = sb("ez", [P, R, L])
        picked = sb("picked", [P, R, L])
        zsum = sb("zsum", [P, R])
        zinv = sb("zinv", [P, R])
        comb = sb("comb", [P, R, L])
        comb_old = sb("comb_old", [P, R - 1, L])
        acc1 = sb("acc1", [P, 2, D])
        hsum = sb("hsum", [P, D])
        hid = sb("hid", [P, D])
        h_hi = sb("h_hi", [P, KD, P], F32R)
        h_lo = sb("h_lo", [P, KD, P], F32R)
        c3_t = sb("c3_t", [L, P])
        acc2 = sb("acc2", [P, 2, D])
        outb = sb("outb", [P, 1, D])

        small_in = sem("small_in")
        x_first = sem("x_first")
        x_rest = sem("x_rest")
        mask_in = sem("mask_in")
        chunk_in = [sem(f"chunk_in{n}") for n in range(STAGES)]
        ident_ready = sem("ident_ready")
        fills_ready = sem("fills_ready")
        tg_ready = sem("tg_ready")
        prep_mm = sem("prep_mm")
        kt_ready = sem("kt_ready")
        qk_ready = sem("qk_ready")
        vb_ready = sem("vb_ready")
        b2g_ready = sem("b2g_ready")
        pu_hi_ready = sem("pu_hi_ready")
        pu_lo_ready = sem("pu_lo_ready")
        w_hi_ready = sem("w_hi_ready")
        w_lo_ready = sem("w_lo_ready")
        t1_done = sem("t1_done")
        scores_done = sem("scores_done")
        pt_done = sem("pt_done")
        pv_done = sem("pv_done")
        t2_done = sem("t2_done")
        z_done = sem("z_done")
        m1_done = sem("m1_done")
        ht_done = sem("ht_done")
        c3t_done = sem("c3t_done")
        bias_done = sem("bias_done")
        m2_done = sem("m2_done")
        xn1t_ready = sem("xn1t_ready")
        probs_ready = sem("probs_ready")
        probst_ready = sem("probst_ready")
        x2hi_ready = sem("x2hi_ready")
        ez_ready = sem("ez_ready")
        hid_ready = sem("hid_ready")
        hhi_ready = sem("hhi_ready")
        c3t_ready = sem("c3t_ready")
        parts1_ready = sem("parts1_ready")
        stats1_ready = sem("stats1_ready")
        xn1_ready = sem("xn1_ready")
        scores_ready = sem("scores_ready")
        inv_ready = sem("inv_ready")
        x1_ready = sem("x1_ready")
        parts2_ready = sem("parts2_ready")
        stats2_ready = sem("stats2_ready")
        xn2_ready = sem("xn2_ready")
        x2lo_ready = sem("x2lo_ready")
        z_read = sem("z_read")
        top_ready = sem("top_ready")
        zs_ready = sem("zs_ready")
        wanted_ready = sem("wanted_ready")
        marked_ready = sem("marked_ready")
        weigh_ready = sem("weigh_ready")
        comb_ready = sem("comb_ready")
        comb_old_ready = sem("comb_old_ready")
        c1_done = sem("c1_done")
        hsum_ready = sem("hsum_ready")
        hlo_ready = sem("hlo_ready")
        start2_ready = sem("start2_ready")
        c2_done = sem("c2_done")
        out_ready = sem("out_ready")
        rstd1_ready = sem("rstd1_ready")
        rstd2_ready = sem("rstd2_ready")
        out_stored = sem("out_stored")

        SMALL = 9
        FIRST = 4
        REST = (TILES - FIRST) // 4
        block = ctx.enter_context(nc.Block())

        def split_chunks():
            for w in range(2):
                for c in range(WCH):
                    for k in range(KD):
                        yield w, (w * WCH + c) * KD + k, k, slice(c * CHUNK, (c + 1) * CHUNK)

        BEFORE = [(-2, True, False, False, False), (-1, True, True, False, False),
                  (0, True, True, True, False), (1, True, True, True, True)]
        AFTER = [(TILES - 2, False, True, True, True), (TILES - 1, False, False, True, True),
                 (TILES, False, False, False, True)]
        LOOP = (2, TILES - 2)

        @block.sync
        def _(sp):
            sp.dma_start(xb[:, 0:FIRST, :], x_rows[:, 0:FIRST, :]).then_inc(x_first, 16)
            sp.dma_start(ctxb[:, :, :], ctx_t.rearrange("(k p) s -> p k s", p=P)).then_inc(small_in, 16)
            sp.dma_start(wkb[:, :, :], wk_t.rearrange("(k p) h -> p k h", p=P)).then_inc(small_in, 16)
            sp.dma_start(wqb[:, :, :], wq.rearrange("(k p) h -> p k h", p=P)).then_inc(small_in, 16)
            sp.dma_start(wvb[:, :, :], wv_t.rearrange("(k p) h -> p k h", p=P)).then_inc(small_in, 16)
            sp.dma_start(pwb[:, :], p_w).then_inc(small_in, 16)
            sp.dma_start(utb[:, :], u_t).then_inc(small_in, 16)
            sp.dma_start(b2b[:, :], b2).then_inc(small_in, 16)
            sp.dma_start(gates[:, 0:1], g_xattn.rearrange("(a n) -> a n", a=1).to_broadcast([P, 1])).then_inc(small_in, 16)
            sp.dma_start(gates[:, 1:2], g_ffn.rearrange("(a n) -> a n", a=1).to_broadcast([P, 1])).then_inc(small_in, 16)
            sp.dma_start(maskb[:, :, :], mask_rows).then_inc(mask_in, 16)
            for w, n, k, cols in split_chunks():
                if n >= STAGES:
                    sp.wait_ge(w_lo_ready, n - STAGES + 1)
                src = (w1_t, w2_t)[w][k * P:(k + 1) * P, cols]
                sp.dma_start(wstage[n % STAGES][:, :], src).then_inc(chunk_in[n % STAGES], 16)
            for n in range(4):
                part = slice(FIRST + n * REST, FIRST + (n + 1) * REST)
                sp.dma_start(xb[:, part, :], x_rows[:, part, :]).then_inc(x_rest, 16)

            def store(o):
                sp.wait_ge(out_ready, o + 1)
                sp.dma_start(out_rows[:, bass.ds(o, 1), :], outb[:, :, :]).then_inc(out_stored, 16)

            store(0)
            with sp.Fori(1, TILES) as o:
                store(o)
            sp.wait_ge(out_stored, 16 * TILES)

        @block.gpsimd
        def _(pool):
            nc.gpsimd.memset(minus_half[:, :], -0.5).then_inc(fills_ready, 1)
            nc.gpsimd.memset(eps[:, :], LN_EPS).then_inc(fills_ready, 1)
            nc.gpsimd.memset(z[:, :, :], LOWEST).then_inc(fills_ready, 1)
            nc.gpsimd.memset(wanted[:, :, :], LOWEST).then_inc(fills_ready, 1)
            nc.gpsimd.memset(ident[:, :], 0.0).then_inc(fills_ready, 1)
            pool.wait_ge(fills_ready, 5)
            nc.gpsimd.affine_select(out=ident[:, :], in_=ident[:, :], compare_op=ALU.not_equal, fill=1.0,
                                    base=0, pattern=[[-1, P]], channel_multiplier=1).then_inc(ident_ready, 1)

            def rstd(n, stats_ready, mv, var, rs, ready):
                pool.wait_ge(stats_ready, n + 1)
                nc.gpsimd.tensor_tensor(var[:, :], mv[:, 1:2], eps[:, :], ALU.add).then_inc(ready, 1)
                pool.wait_ge(ready, 2 * n + 1)
                nc.gpsimd.tensor_tensor(rs[:, :], var[:, :], minus_half[:, :], ALU.pow).then_inc(ready, 1)

            def first_norm(m):
                rstd(m, stats1_ready, mv1, var1, rstd1, rstd1_ready)

            def second_norm(n):
                rstd(n, stats2_ready, mv2, var2, rstd2, rstd2_ready)

            first_norm(0)
            first_norm(1)
            second_norm(0)
            with pool.Fori(1, TILES - 1) as n:
                first_norm(n + 1)
                second_norm(n)
            second_norm(TILES - 1)

        @block.scalar
        def _(act):
            act.wait_ge(small_in, 16 * SMALL)
            nc.scalar.activation(tg[:, :], gates[:, :], ACT.Tanh).then_inc(tg_ready, 1)
            act.wait_ge(prep_mm, 1)
            for m in range(KD):
                nc.scalar.activation(kt[:, m, :], ring[:, m, 0:B * SC], ACT.Copy).then_inc(kt_ready, 1)
            act.wait_ge(tg_ready, 1)
            act.wait_ge(prep_mm, 2)
            for b in range(B):
                src = ring[0:SC, 2 + b // 2, (b % 2) * D:(b % 2 + 1) * D]
                nc.scalar.activation(vb[:, b, :], src, ACT.Copy, scale=tg[0:SC, 0:1]).then_inc(vb_ready, 1)
            nc.scalar.activation(b2g[:, :], b2b[:, :], ACT.Copy, scale=tg[0:L, 1:2]).then_inc(b2g_ready, 1)
            act.wait_ge(prep_mm, 3)
            nc.scalar.activation(pu_hi[:, :, :], bias_ps[:, 0:KD * R * L].rearrange("p (k n) -> p k n", k=KD),
                                 ACT.Copy).then_inc(pu_hi_ready, 1)
            act.wait_ge(prep_mm, 4)
            for m in range(KD):
                src = (att_ps, hturn_ps)[m][:, 0:B * SC]
                nc.scalar.activation(qk[:, m, :], src, ACT.Copy, scale=SCALE).then_inc(qk_ready, 1)

            def split_high(weight):
                for w, n, k, cols in split_chunks():
                    if w == weight:
                        act.wait_ge(chunk_in[n % STAGES], 16 * (n // STAGES + 1))
                        dst = (w1_hi, w2_hi)[w][:, k, cols]
                        gate = 1.0 if w == 0 else tg[:, 1:2]
                        nc.scalar.activation(dst, wstage[n % STAGES][:, :], ACT.Copy, scale=gate).then_inc(w_hi_ready, 1)

            def step(i, norm, attend, first, second):
                n, o = i + 1, i - 1
                if second:
                    act.wait_ge(ht_done, o + 1)
                    nc.scalar.activation(h_hi[:, :, :], hturn_ps[:, 0:D].rearrange("p (k t) -> p k t", k=KD),
                                         ACT.Copy).then_inc(hhi_ready, 1)
                if attend:
                    act.wait_ge(t1_done, n + 1)
                    nc.scalar.activation(xn1_t[:, :, :], turn_ps[:, 0:D].rearrange("p (k t) -> p k t", k=KD),
                                         ACT.Copy).then_inc(xn1t_ready, 1)
                if second:
                    act.wait_ge(c3t_done, o + 1)
                    nc.scalar.activation(c3_t[:, :], bias_ps[0:L, 0:P], ACT.Copy).then_inc(c3t_ready, 1)
                if attend:
                    act.wait_ge(scores_ready, 2 * n + 2)
                    nc.scalar.activation(probs[:, :], scores[:, :], ACT.Exp, bias=neg_max[:, 0:1],
                                         accum_out=row_sum[:, 0:1]).then_inc(probs_ready, 1)
                    act.wait_ge(pt_done, n + 1)
                    nc.scalar.activation(probs_t[:, :], turn_ps[0:SC, 0:P], ACT.Copy).then_inc(probst_ready, 1)
                if first:
                    act.wait_ge(hsum_ready, i + 1)
                    nc.scalar.activation(hid[:, :], hsum[:, :], ACT.Gelu).then_inc(hid_ready, 1)
                if attend:
                    act.wait_ge(t2_done, n + 1)
                    nc.scalar.activation(x2_hi[:, :, :], turn_ps[:, 0:D].rearrange("p (k t) -> p k t", k=KD),
                                         ACT.Copy).then_inc(x2hi_ready, 1)
                    act.wait_ge(zs_ready, n + 1)
                    nc.scalar.activation(ez[:, :, :], zs[:, :, :], ACT.Exp).then_inc(ez_ready, 1)

            step(*BEFORE[0])
            step(*BEFORE[1])
            split_high(0)
            step(*BEFORE[2])
            split_high(1)
            step(*BEFORE[3])
            with act.Fori(*LOOP) as i:
                step(i, True, True, True, True)
            for args in AFTER:
                step(*args)

        @block.vector
        def _(dve):
            dve.wait_ge(pu_hi_ready, 1)
            nc.vector.tensor_tensor(pu_lo[:, :, :], bias_ps[:, 0:KD * R * L].rearrange("p (k n) -> p k n", k=KD),
                                    pu_hi[:, :, :].bitcast(F32), ALU.subtract).then_inc(pu_lo_ready, 1)

            def split_low(weight):
                for w, n, k, cols in split_chunks():
                    if w == weight:
                        dve.wait_ge(w_hi_ready, n + 1)
                        src = wstage[n % STAGES][:, :]
                        hi = (w1_hi, w2_hi)[w][:, k, cols].bitcast(F32)
                        lo = (w1_lo, w2_lo)[w][:, k, cols]
                        if w == 0:
                            nc.vector.tensor_tensor(lo, src, hi, ALU.subtract).then_inc(w_lo_ready, 1)
                        else:
                            nc.vector.scalar_tensor_tensor(lo, src, tg[:, 1:2], hi, ALU.mult,
                                                           ALU.subtract).then_inc(w_lo_ready, 1)

            def combine1(i, pair, halves=(0, 1)):
                if 0 in halves:
                    dve.wait_ge(m1_done, PAIRS * i + pair + 1)
                for e in (2 * pair + h for h in halves):
                    half = e % 2
                    product = ring[:, pair % RING, half * D:(half + 1) * D]
                    weight = comb[:, 0, e:e + 1]
                    if pair == 0:
                        ins = nc.vector.tensor_scalar(acc1[:, half, :], product, weight, None, ALU.mult)
                    else:
                        dve.wait_ge(c1_done, L * i + e - 1)
                        ins = nc.vector.scalar_tensor_tensor(acc1[:, half, :], product, weight, acc1[:, half, :],
                                                             ALU.mult, ALU.add)
                    ins.then_inc(c1_done, 1)

            def combine2(o, pair, halves=(0, 1)):
                if 0 in halves:
                    dve.wait_ge(m2_done, PAIRS * o + pair + 1)
                for e in (2 * pair + h for h in halves):
                    half = e % 2
                    product = ring[:, (PAIRS + pair) % RING, half * D:(half + 1) * D]
                    weight = comb_old[:, 0, e:e + 1]
                    if e == 1:
                        ins = nc.vector.tensor_scalar(acc2[:, half, :], product, weight, None, ALU.mult)
                    else:
                        if e == 0:
                            dve.wait_ge(start2_ready, o + 1)
                        else:
                            dve.wait_ge(c2_done, L * o + e - 1)
                        ins = nc.vector.scalar_tensor_tensor(acc2[:, half, :], product, weight, acc2[:, half, :],
                                                             ALU.mult, ALU.add)
                    ins.then_inc(c2_done, 1)

            def xtile(t):
                return xb[:, bass.ds(t, 1), :].rearrange("p a d -> p (a d)")

            def step(i, norm, attend, first, second):
                m, n, o = i + 2, i + 1, i - 1

                def one(*halves):
                    if first:
                        combine1(i, *halves)

                def two(*halves):
                    if second:
                        combine2(o, *halves)

                if first:
                    dve.wait_ge(comb_ready, i + 1)
                one(0)
                if second:
                    dve.wait_ge(hhi_ready, o + 1)
                    nc.vector.tensor_tensor(h_lo[:, :, :], hturn_ps[:, 0:D].rearrange("p (k t) -> p k t", k=KD),
                                            h_hi[:, :, :].bitcast(F32), ALU.subtract).then_inc(hlo_ready, 1)
                one(1)
                if attend:
                    dve.wait_ge(scores_done, n + 1)
                    nc.vector.tensor_tensor(scores[:, :], att_ps[:, 0:SC],
                                            maskb[:, bass.ds(n, 1), :].rearrange("p a s -> p (a s)"),
                                            ALU.add).then_inc(scores_ready, 1)
                one(2, (0,))
                if attend:
                    dve.wait_ge(scores_ready, 2 * n + 1)
                    nc.vector.tensor_reduce(neg_max[:, 0:1], scores[:, :], AX.X, ALU.max,
                                            negate=True).then_inc(scores_ready, 1)
                one(2, (1,))
                if norm:
                    nc.vector.bn_stats(stats1[:, :], xtile(m)).then_inc(parts1_ready, 1)
                    dve.wait_ge(parts1_ready, m + 1)
                one(3, (0,))
                if norm:
                    nc.vector.bn_aggr(mv1[:, :], stats1[:, :]).then_inc(stats1_ready, 1)
                one(3, (1,))
                if attend:
                    dve.wait_ge(probs_ready, n + 1)
                    nc.vector.reciprocal(inv_sum[:, 0:1], row_sum[:, 0:1]).then_inc(inv_ready, 1)
                if second:
                    dve.wait_ge(bias_done, o + 1)
                    nc.vector.tensor_tensor(acc2[:, 0, :], bias_ps[:, D:2 * D], xtile(o),
                                            ALU.add).then_inc(start2_ready, 1)
                one(4)
                if norm:
                    dve.wait_ge(rstd1_ready, 2 * m + 2)
                    nc.vector.tensor_scalar(xn1[:, :], xtile(m), mv1[:, 0:1], rstd1[:, 0:1], ALU.subtract,
                                            ALU.mult).then_inc(xn1_ready, 1)
                if attend:
                    dve.wait_ge(inv_ready, n + 1)
                    dve.wait_ge(pv_done, n + 1)
                    nc.vector.scalar_tensor_tensor(xtile(n), att_ps[:, D:2 * D], inv_sum[:, 0:1], xtile(n),
                                                   ALU.mult, ALU.add).then_inc(x1_ready, 1)
                    dve.wait_ge(x1_ready, n + 1)
                one(5, (0,))
                if attend:
                    nc.vector.bn_stats(stats2[:, :], xtile(n)).then_inc(parts2_ready, 1)
                    dve.wait_ge(parts2_ready, n + 1)
                one(5, (1,))
                if attend:
                    nc.vector.bn_aggr(mv2[:, :], stats2[:, :]).then_inc(stats2_ready, 1)
                if first:
                    dve.wait_ge(c1_done, L * (i + 1))
                    nc.vector.tensor_tensor(hsum[:, :], acc1[:, 0, :], acc1[:, 1, :],
                                            ALU.add).then_inc(hsum_ready, 1)
                two(0, (0,))
                if attend:
                    dve.wait_ge(rstd2_ready, 2 * n + 2)
                    nc.vector.tensor_scalar(xn2[:, :], xtile(n), mv2[:, 0:1], rstd2[:, 0:1], ALU.subtract,
                                            ALU.mult).then_inc(xn2_ready, 1)
                two(0, (1,))
                two(1)
                two(2, (0,))
                if attend:
                    dve.wait_ge(x2hi_ready, n + 1)
                    nc.vector.tensor_tensor(x2_lo[:, :, :], turn_ps[:, 0:D].rearrange("p (k t) -> p k t", k=KD),
                                            x2_hi[:, :, :].bitcast(F32), ALU.subtract).then_inc(x2lo_ready, 1)
                two(2, (1,))
                two(3, (0,))
                if attend:
                    dve.wait_ge(z_done, n + 1)
                    nc.vector.tensor_copy(z[:, :, 0:L], att_ps[:, 128:128 + R * L].rearrange("p (r e) -> p r e", r=R)
                                          ).then_inc(z_read, 1)
                two(3, (1,))
                if attend:
                    dve.wait_ge(fills_ready, 5)
                    dve.wait_ge(z_read, n + 1)
                    for r in range(R):
                        nc.vector.max(top[:, r, :], z[:, r, 0:L]).then_inc(top_ready, 1)
                two(4, (0,))
                if attend:
                    dve.wait_ge(top_ready, R * (n + 1))
                    nc.vector.tensor_tensor(zs[:, :, :], z[:, :, 0:L], top[:, :, 0:1].to_broadcast([P, R, L]),
                                            ALU.subtract).then_inc(zs_ready, 1)
                    nc.vector.tensor_copy(wanted[:, :, 0:TOPK], top[:, :, 0:TOPK]).then_inc(wanted_ready, 1)
                two(4, (1,))
                if attend:
                    dve.wait_ge(fills_ready, 5)
                    dve.wait_ge(wanted_ready, n + 1)
                    for r in range(R):
                        nc.vector.match_replace(marked[:, r, :], wanted[:, r, :], z[:, r, :],
                                                PICKED).then_inc(marked_ready, 1)
                two(5, (0,))
                if attend:
                    dve.wait_ge(marked_ready, R * (n + 1))
                    dve.wait_ge(ez_ready, n + 1)
                    nc.vector.scalar_tensor_tensor(picked[:, :, :], marked[:, :, 0:L], PICKED, ez[:, :, :],
                                                   ALU.is_equal, ALU.mult).then_inc(weigh_ready, 1)
                two(5, (1,))
                if attend:
                    dve.wait_ge(weigh_ready, 3 * n + 1)
                    nc.vector.tensor_reduce(zsum[:, :], picked[:, :, :], AX.X, ALU.add).then_inc(weigh_ready, 1)
                if second:
                    dve.wait_ge(c2_done, L * (o + 1))
                    if not (type(o) is int and o == 0):
                        dve.wait_ge(out_stored, 16 * o)
                    nc.vector.tensor_tensor(outb[:, 0, :], acc2[:, 0, :], acc2[:, 1, :],
                                            ALU.add).then_inc(out_ready, 1)
                if first:
                    nc.vector.tensor_copy(comb_old[:, :, :], comb[:, 1:R, :]).then_inc(comb_old_ready, 1)
                if attend:
                    dve.wait_ge(weigh_ready, 3 * n + 2)
                    nc.vector.reciprocal(zinv[:, :], zsum[:, :]).then_inc(weigh_ready, 1)
                if attend:
                    dve.wait_ge(weigh_ready, 3 * n + 3)
                    nc.vector.tensor_tensor(comb[:, :, :], picked[:, :, :],
                                            zinv[:, :].rearrange("p (r a) -> p r a", a=1).to_broadcast([P, R, L]),
                                            ALU.mult).then_inc(comb_ready, 1)

            dve.wait_ge(x_first, 16)
            dve.wait_ge(mask_in, 16)
            dve.wait_ge(fills_ready, 5)
            step(*BEFORE[0])
            step(*BEFORE[1])
            split_low(0)
            step(*BEFORE[2])
            split_low(1)
            dve.wait_ge(x_rest, 64)
            step(*BEFORE[3])
            with dve.Fori(*LOOP) as i:
                step(i, True, True, True, True)
            for args in AFTER:
                step(*args)

        @block.tensor
        def _(pe):
            pe.wait_ge(small_in, 16 * SMALL)
            for m in range(KD):
                for k in range(KD):
                    mm = nc.tensor.matmul(ring[:, m, 0:B * SC], wkb[:, k, m * P:(m + 1) * P], ctxb[:, k, :],
                                          start=k == 0, stop=k == KD - 1)
            mm.then_inc(prep_mm, 1)
            for b in range(B):
                for k in range(KD):
                    mm = nc.tensor.matmul(ring[0:SC, 2 + b // 2, (b % 2) * D:(b % 2 + 1) * D],
                                          ctxb[:, k, b * SC:(b + 1) * SC], wvb[:, k, :],
                                          start=k == 0, stop=k == KD - 1)
            mm.then_inc(prep_mm, 1)
            for m in range(KD):
                mm = nc.tensor.matmul(bias_ps[:, m * R * L:(m + 1) * R * L], pwb[:, m * P:(m + 1) * P], utb[:, :],
                                      start=True, stop=True)
            mm.then_inc(prep_mm, 1)
            pe.wait_ge(kt_ready, KD)
            for m in range(KD):
                for k in range(KD):
                    mm = nc.tensor.matmul((att_ps, hturn_ps)[m][:, 0:B * SC], wqb[:, k, m * P:(m + 1) * P],
                                          kt[:, k, :], start=k == 0, stop=k == KD - 1)
            mm.then_inc(prep_mm, 1)
            pe.wait_ge(ident_ready, 1)
            pe.wait_ge(qk_ready, KD)
            pe.wait_ge(vb_ready, B)
            pe.wait_ge(b2g_ready, 1)
            pe.wait_ge(pu_lo_ready, 1)

            def turn(dst, src):
                return nc.tensor.transpose(dst, src, ident[0:src.shape[0], 0:src.shape[0]])

            def three_passes(dst, a_hi, a_lo, w_hi, w_lo, cols):
                for k in range(KD):
                    nc.tensor.matmul(dst, a_hi[:, k, :], w_hi[:, k, cols], start=k == 0, stop=False)
                    nc.tensor.matmul(dst, a_hi[:, k, :], w_lo[:, k, cols], start=False, stop=False)
                    mm = nc.tensor.matmul(dst, a_lo[:, k, :], w_hi[:, k, cols], start=False, stop=k == KD - 1)
                return mm

            def mixture1(i, pair, beside_second, settle):
                if pair >= RING:
                    pe.wait_ge(c1_done, L * i + 2 * (pair - RING) + 2)
                elif beside_second:
                    pe.wait_ge(c2_done, L * (i - 2) + 2 * (pair + 2) + 2)
                elif settle:
                    pe.wait_ge(c1_done, L * i)
                three_passes(ring[:, pair % RING, :], x2_hi, x2_lo, w1_hi, w1_lo,
                             slice(2 * pair * D, 2 * (pair + 1) * D)).then_inc(m1_done, 1)

            def mixture2(o, pair, beside_first):
                if pair >= RING:
                    pe.wait_ge(c2_done, L * o + 2 * (pair - RING) + 2)
                elif beside_first:
                    pe.wait_ge(c1_done, L * (o + 1) + 2 * (pair + 2) + 2)
                else:
                    pe.wait_ge(c2_done, L * o)
                three_passes(ring[:, (PAIRS + pair) % RING, :], h_hi, h_lo, w2_hi, w2_lo,
                             slice(2 * pair * D, 2 * (pair + 1) * D)).then_inc(m2_done, 1)

            def step(i, norm, attend, first, second):
                n, o = i + 1, i - 1
                after_first = not (type(i) is int and i < 2)
                def m1(pair):
                    if first:
                        mixture1(i, pair, after_first, type(i) is int and i == 1)

                def m2(pair):
                    if second:
                        mixture2(o, pair, first)

                m1(0)
                if second:
                    pe.wait_ge(hid_ready, o + 1)
                    for k in range(KD):
                        mm = turn(hturn_ps[:, k * P:(k + 1) * P], hid[:, k * P:(k + 1) * P])
                    mm.then_inc(ht_done, 1)
                if attend:
                    pe.wait_ge(xn1_ready, n + 1)
                    for k in range(KD):
                        mm = turn(turn_ps[:, k * P:(k + 1) * P], xn1[:, k * P:(k + 1) * P])
                    mm.then_inc(t1_done, 1)
                if second:
                    pe.wait_ge(comb_old_ready, o + 1)
                    turn(bias_ps[0:L, 0:P], comb_old[:, 1, :]).then_inc(c3t_done, 1)
                m1(1)
                if attend:
                    pe.wait_ge(xn1t_ready, n + 1)
                    if not (type(n) is int and n == 0):
                        pe.wait_ge(z_read, n)
                    for k in range(KD):
                        mm = nc.tensor.matmul(att_ps[:, 0:SC], xn1_t[:, k, :],
                                              qk[:, k, bass.ds((n // TPB) * SC, SC)],
                                              start=k == 0, stop=k == KD - 1)
                    mm.then_inc(scores_done, 1)
                m1(2)
                m1(3)
                if attend:
                    pe.wait_ge(probs_ready, n + 1)
                    turn(turn_ps[0:SC, 0:P], probs[:, :]).then_inc(pt_done, 1)
                if second:
                    pe.wait_ge(c3t_ready, o + 1)
                    nc.tensor.matmul(bias_ps[:, D:2 * D], c3_t[:, :], b2g[:, :], start=True,
                                     stop=True).then_inc(bias_done, 1)
                m1(4)
                if attend:
                    pe.wait_ge(probst_ready, n + 1)
                    nc.tensor.matmul(att_ps[:, D:2 * D], probs_t[:, :],
                                     vb[:, bass.ds(n // TPB, 1), :].rearrange("s a d -> s (a d)"),
                                     start=True, stop=True).then_inc(pv_done, 1)
                m1(5)
                if second:
                    pe.wait_ge(hlo_ready, o + 1)
                m2(0)
                m2(1)
                if attend:
                    pe.wait_ge(xn2_ready, n + 1)
                    for k in range(KD):
                        mm = turn(turn_ps[:, k * P:(k + 1) * P], xn2[:, k * P:(k + 1) * P])
                    mm.then_inc(t2_done, 1)
                m2(2)
                m2(3)
                if attend:
                    pe.wait_ge(x2lo_ready, n + 1)
                    three_passes(att_ps[:, 128:128 + R * L], x2_hi, x2_lo, pu_hi, pu_lo,
                                 slice(0, R * L)).then_inc(z_done, 1)
                m2(4)
                m2(5)

            step(*BEFORE[1])
            pe.wait_ge(w_lo_ready, NCH)
            step(*BEFORE[2])
            pe.wait_ge(w_lo_ready, 2 * NCH)
            step(*BEFORE[3])
            with pe.Fori(*LOOP) as i:
                step(i, True, True, True, True)
            for args in AFTER:
                step(*args)


def kernel(**inputs):
    import numpy as np
    import concourse.bacc as bacc
    from concourse.bass_utils import run_bass_kernel_spmd

    def turned(a):
        return np.ascontiguousarray(np.asarray(a).T)

    ctx = np.asarray(inputs["ctx_1024"])
    w1, w2 = np.asarray(inputs["L0_ffn_W1"]), np.asarray(inputs["L0_ffn_W2"])
    u = np.concatenate([np.asarray(inputs[f"L0_ffn_U{n}"]) for n in (1, 2, 3)], axis=0)
    arrays = {
        "x": np.ascontiguousarray(inputs["x"]),
        "ctx_t": turned(ctx.reshape(-1, ctx.shape[2])),
        "mask": np.ascontiguousarray(inputs["mask_BxSxS2_ff0"]),
        "g_xattn": np.ascontiguousarray(inputs["g_xattn"]),
        "g_ffn": np.ascontiguousarray(inputs["g_ffn"]),
        "wq": np.ascontiguousarray(inputs["L0_xattn_Wq"]),
        "wk_t": turned(inputs["L0_xattn_Wk"]),
        "wv_t": turned(inputs["L0_xattn_Wv"]),
        "p_w": np.ascontiguousarray(inputs["L0_ffn_P_w"]),
        "u_t": turned(u),
        "w1_t": turned(w1.reshape(-1, w1.shape[2])),
        "w2_t": turned(w2.reshape(-1, w2.shape[2])),
        "b2": np.ascontiguousarray(inputs["L0_ffn_b2"]),
    }
    nc = bacc.Bacc("TRN2", target_bir_lowering=False, num_devices=1)
    feeds, args = {}, []
    for name, a in arrays.items():
        feeds[f"in_{name}"] = a
        args.append(nc.dram_tensor(f"in_{name}", a.shape, mybir.dt.from_np(a.dtype), kind="ExternalInput").ap())
    out = nc.dram_tensor("out", arrays["x"].shape, F32, kind="ExternalOutput").ap()
    gated_xattn_and_routed_ffn(nc, *args, out)
    result = run_bass_kernel_spmd(nc, [feeds], core_ids=[0])
    return result.results[0]["out"]
```

```python
from contextlib import ExitStack

import concourse.bass as bass
from concourse import mybir

F32 = mybir.dt.float32
F32R = mybir.dt.float32r
ALU = mybir.AluOpType
ACT = mybir.ActivationFunctionType
AX = mybir.AxisListType

LN_EPS = 1e-5
LOWEST = -3.4028234663852886e38
PICKED = 3.4028234663852886e38


def gated_xattn_and_routed_ffn(nc, x, ctx_t, mask_t, g_xattn, g_ffn, wq, wk_t, wv_t, p_w, u_t, w1_t, w2_t, b2, out):
    P = 128
    B, S, D = x.shape
    SC = mask_t.shape[2]
    L = b2.shape[0]
    KD = D // P
    TILES = B * S // P
    TPB = S // P
    R = 3
    TOPK = 3
    ZW = L + 8 - TOPK
    PAIRS = L // 2
    RING = 4
    STAGES = 6
    Q = 32
    ADDR = p_w.shape[0]
    SCALE = 1.0 / float(D) ** 0.5
    BN = nc.vector.BN_STATS_DIM
    assert D == KD * P == 256 and L % 2 == 0 and 2 * D == 512 and S % P == 0

    x_rows = x.rearrange("b (n p) d -> p (b n) d", p=P)
    out_rows = out.rearrange("b (n p) d -> p (b n) d", p=P)

    with ExitStack() as ctx:
        def sb(name, shape, dt=F32):
            return ctx.enter_context(nc.sbuf_tensor(name, shape, dt))

        def ps(name, shape):
            return ctx.enter_context(nc.psum_tensor(name, shape, F32))

        def sem(name):
            return ctx.enter_context(nc.semaphore(name))

        ring = ps("ring", [P, RING, 2 * D])
        turn_ps = ps("turn_ps", [P, 2 * D])
        hturn_ps = ps("hturn_ps", [P, 2 * D])
        att_ps = ps("att_ps", [P, 2 * D])
        bias_ps = ps("bias_ps", [P, 2 * D])

        xb = sb("xb", [P, TILES, D])
        maskb = sb("maskb", [P, TILES, SC])
        ident = sb("ident", [P, P])
        minus_half = sb("minus_half", [P, 1])
        eps = sb("eps", [P, 1])
        ctxb = sb("ctxb", [P, KD, B * SC])
        wqb = sb("wqb", [P, KD, D])
        wkb = sb("wkb", [P, KD, D])
        wvb = sb("wvb", [P, KD, D])
        pwb = sb("pwb", [ADDR, D])
        utb = sb("utb", [ADDR, R * L])
        b2b = sb("b2b", [3 * Q, D])
        gates = sb("gates", [P, 2])
        tg = sb("tg", [P, 2])
        b2g = sb("b2g", [3 * Q, D], F32R)
        b2g_tmp = sb("b2g_tmp", [3 * Q, D], F32R)
        kt = sb("kt", [P, KD, B * SC])
        qk = sb("qk", [P, KD, B * SC])
        vb = sb("vb", [SC, B, D])
        pu = sb("pu", [P, KD, R * L])
        wstage = sb("wstage", [P, STAGES, KD, 2 * D])
        w1_hi = sb("w1_hi", [P, KD, L * D], F32R)
        w1_lo = sb("w1_lo", [P, KD, L * D], F32R)
        w2_hi = sb("w2_hi", [P, KD, L * D], F32R)
        w2_lo = sb("w2_lo", [P, KD, L * D], F32R)

        stats1 = sb("stats1", [P, BN])
        mv1 = sb("mv1", [P, 2])
        var1 = sb("var1", [P, 1])
        rstd1 = sb("rstd1", [P, 1])
        xn1 = sb("xn1", [P, D])
        xn1_t = sb("xn1_t", [P, KD, P])
        scores = sb("scores", [P, SC])
        neg_max = sb("neg_max", [P, 1])
        probs = sb("probs", [P, SC])
        row_sum = sb("row_sum", [P, 1])
        inv_sum = sb("inv_sum", [P, 1])
        probs_t = sb("probs_t", [SC, P])
        stats2 = sb("stats2", [P, BN])
        mv2 = sb("mv2", [P, 2])
        var2 = sb("var2", [P, 1])
        rstd2 = sb("rstd2", [P, 1])
        xn2 = sb("xn2", [P, D])
        x2_t = sb("x2_t", [P, KD, P])
        x2_hi = sb("x2_hi", [P, KD, P], F32R)
        x2_lo = sb("x2_lo", [P, KD, P], F32R)
        z = sb("z", [P, R, ZW])
        top = sb("top", [P, R, 8])
        wanted = sb("wanted", [P, R, 8])
        marked = sb("marked", [P, R, ZW])
        zs = sb("zs", [P, R, L])
        ez = sb("ez", [P, R, L])
        picked = sb("picked", [P, R, L])
        zsum = sb("zsum", [P, R])
        zinv = sb("zinv", [P, R])
        comb = sb("comb", [P, R, L])
        comb_old = sb("comb_old", [P, L])
        acc1 = sb("acc1", [P, 2, D])
        hsum = sb("hsum", [P, D])
        hid = sb("hid", [P, D])
        h_hi = sb("h_hi", [P, KD, P], F32R)
        h_lo = sb("h_lo", [P, KD, P], F32R)
        c3_parts = sb("c3_parts", [P, 3, Q], F32R)
        c3_t = sb("c3_t", [3 * Q, P], F32R)
        acc2 = sb("acc2", [P, 2, D])
        outb = sb("outb", [P, 1, D])

        wk_in = sem("wk_in")
        wq_in = sem("wq_in")
        wv_in = sem("wv_in")
        gates_in = sem("gates_in")
        route_in = sem("route_in")
        b2_in = sem("b2_in")
        x_first = sem("x_first")
        x_second = sem("x_second")
        x_rest = sem("x_rest")
        mask_first = sem("mask_first")
        mask_rest = sem("mask_rest")
        pair_in = [sem(f"pair_in{c}") for c in range(2 * PAIRS)]
        ident_ready = sem("ident_ready")
        fills_ready = sem("fills_ready")
        tg_ready = sem("tg_ready")
        kt_done = sem("kt_done")
        qk_done = sem("qk_done")
        v_done = sem("v_done")
        pu_done = sem("pu_done")
        kt_ready = sem("kt_ready")
        qk_ready = sem("qk_ready")
        vb_ready = sem("vb_ready")
        b2g_ready = sem("b2g_ready")
        pu_ready = sem("pu_ready")
        w_hi_ready = sem("w_hi_ready")
        w_lo_ready = sem("w_lo_ready")
        t1_done = sem("t1_done")
        scores_done = sem("scores_done")
        pt_done = sem("pt_done")
        pv_done = sem("pv_done")
        t2_done = sem("t2_done")
        z_done = sem("z_done")
        m1_done = sem("m1_done")
        ht_done = sem("ht_done")
        c3t_done = sem("c3t_done")
        bias_done = sem("bias_done")
        m2_done = sem("m2_done")
        xn1t_ready = sem("xn1t_ready")
        probs_ready = sem("probs_ready")
        probst_ready = sem("probst_ready")
        x2t_ready = sem("x2t_ready")
        x2hi_ready = sem("x2hi_ready")
        ez_ready = sem("ez_ready")
        hid_ready = sem("hid_ready")
        hhi_ready = sem("hhi_ready")
        c3hi_ready = sem("c3hi_ready")
        c3t_ready = sem("c3t_ready")
        parts1_ready = sem("parts1_ready")
        stats1_ready = sem("stats1_ready")
        xn1_ready = sem("xn1_ready")
        scores_ready = sem("scores_ready")
        inv_ready = sem("inv_ready")
        x1_ready = sem("x1_ready")
        parts2_ready = sem("parts2_ready")
        stats2_ready = sem("stats2_ready")
        xn2_ready = sem("xn2_ready")
        x2lo_ready = sem("x2lo_ready")
        z_read = sem("z_read")
        top_ready = sem("top_ready")
        zs_ready = sem("zs_ready")
        wanted_ready = sem("wanted_ready")
        marked_ready = sem("marked_ready")
        weigh_ready = sem("weigh_ready")
        comb_ready = sem("comb_ready")
        comb_old_ready = sem("comb_old_ready")
        c1_done = sem("c1_done")
        hsum_ready = sem("hsum_ready")
        hlo_ready = sem("hlo_ready")
        c3lo_ready = sem("c3lo_ready")
        b2glo_ready = sem("b2glo_ready")
        start2_ready = sem("start2_ready")
        c2_done = sem("c2_done")
        out_ready = sem("out_ready")
        rstd1_ready = sem("rstd1_ready")
        rstd2_ready = sem("rstd2_ready")
        out_stored = sem("out_stored")

        FIRST, SECOND = 2, 4
        REST = (TILES - SECOND) // 4
        block = ctx.enter_context(nc.Block())

        def pair_cols(c):
            return slice((c % PAIRS) * 2 * D, (c % PAIRS + 1) * 2 * D)

        BEFORE = [(-2, True, False, False, False), (-1, True, True, False, False),
                  (0, True, True, True, False), (1, True, True, True, True)]
        AFTER = [(TILES - 2, False, True, True, True), (TILES - 1, False, False, True, True),
                 (TILES, False, False, False, True)]
        LOOP = (2, TILES - 2)
        SPREAD = {0: 0, 1: 1, 3: 2, 5: 3, 6: 4, 7: 5}

        @block.sync
        def _(sp):
            def load_pair(c):
                src = (w1_t, w2_t)[c // PAIRS].rearrange("(k p) n -> p k n", p=P)[:, :, pair_cols(c)]
                if c >= STAGES:
                    sp.wait_ge(w_lo_ready, c - STAGES + 1)
                sp.dma_start(wstage[:, c % STAGES], src).then_inc(pair_in[c], 16)

            sp.dma_start(ctxb[:, :, :], ctx_t.rearrange("(k p) s -> p k s", p=P)).then_inc(wk_in, 16)
            sp.dma_start(wkb[:, :, :], wk_t.rearrange("(k p) h -> p k h", p=P)).then_inc(wk_in, 16)
            sp.dma_start(wqb[:, :, :], wq.rearrange("(k p) h -> p k h", p=P)).then_inc(wq_in, 16)
            sp.dma_start(xb[:, 0:FIRST, :], x_rows[:, 0:FIRST, :]).then_inc(x_first, 16)
            load_pair(0)
            sp.dma_start(maskb[:, 0:FIRST, :], mask_t[:, 0:FIRST, :]).then_inc(mask_first, 16)
            sp.dma_start(wvb[:, :, :], wv_t.rearrange("(k p) h -> p k h", p=P)).then_inc(wv_in, 16)
            sp.dma_start(gates[:, 0:1], g_xattn.rearrange("(a n) -> a n", a=1).to_broadcast([P, 1])).then_inc(gates_in, 16)
            sp.dma_start(gates[:, 1:2], g_ffn.rearrange("(a n) -> a n", a=1).to_broadcast([P, 1])).then_inc(gates_in, 16)
            load_pair(1)
            sp.dma_start(pwb[:, :], p_w).then_inc(route_in, 16)
            sp.dma_start(utb[:, :], u_t).then_inc(route_in, 16)
            load_pair(2)
            for n in range(3):
                sp.dma_start(b2b[n * Q:n * Q + L, :], b2).then_inc(b2_in, 16)
            for c in range(3, PAIRS):
                load_pair(c)
            sp.dma_start(xb[:, FIRST:SECOND, :], x_rows[:, FIRST:SECOND, :]).then_inc(x_second, 16)
            for c in range(PAIRS, 2 * PAIRS):
                load_pair(c)
            sp.dma_start(maskb[:, FIRST:TILES, :], mask_t[:, FIRST:TILES, :]).then_inc(mask_rest, 16)
            for n in range(4):
                part = slice(SECOND + n * REST, SECOND + (n + 1) * REST)
                sp.dma_start(xb[:, part, :], x_rows[:, part, :]).then_inc(x_rest, 16)

            def store(o):
                sp.wait_ge(out_ready, o + 1)
                sp.dma_start(out_rows[:, bass.ds(o, 1), :], outb[:, :, :]).then_inc(out_stored, 16)

            store(0)
            with sp.Fori(1, TILES) as o:
                store(o)
            sp.wait_ge(out_stored, 16 * TILES)

        @block.gpsimd
        def _(pool):
            nc.gpsimd.memset(minus_half[:, :], -0.5).then_inc(fills_ready, 1)
            nc.gpsimd.memset(eps[:, :], LN_EPS).then_inc(fills_ready, 1)
            nc.gpsimd.memset(z[:, :, :], LOWEST).then_inc(fills_ready, 1)
            nc.gpsimd.memset(wanted[:, :, :], LOWEST).then_inc(fills_ready, 1)
            nc.gpsimd.memset(ident[:, :], 0.0).then_inc(fills_ready, 1)
            nc.gpsimd.memset(c3_parts[:, :, :].bitcast(F32), 0.0).then_inc(fills_ready, 1)
            nc.gpsimd.memset(b2g[:, :].bitcast(F32), 0.0).then_inc(fills_ready, 1)
            pool.wait_ge(fills_ready, 5)
            nc.gpsimd.affine_select(out=ident[:, :], in_=ident[:, :], compare_op=ALU.not_equal, fill=1.0,
                                    base=0, pattern=[[-1, P]], channel_multiplier=1).then_inc(ident_ready, 1)

            def rstd(n, stats_ready, mv, var, rs, ready):
                pool.wait_ge(stats_ready, n + 1)
                nc.gpsimd.tensor_tensor(var[:, :], mv[:, 1:2], eps[:, :], ALU.add).then_inc(ready, 1)
                pool.wait_ge(ready, 2 * n + 1)
                nc.gpsimd.tensor_tensor(rs[:, :], var[:, :], minus_half[:, :], ALU.pow).then_inc(ready, 1)

            def first_norm(m):
                rstd(m, stats1_ready, mv1, var1, rstd1, rstd1_ready)

            def second_norm(n):
                rstd(n, stats2_ready, mv2, var2, rstd2, rstd2_ready)

            first_norm(0)
            first_norm(1)
            second_norm(0)
            with pool.Fori(1, TILES - 1) as n:
                first_norm(n + 1)
                second_norm(n)
            second_norm(TILES - 1)

        @block.scalar
        def _(act):
            def gate_values(b):
                act.wait_ge(v_done, b + 1)
                src = ring[0:SC, b, 0:D]
                nc.scalar.activation(vb[:, b, :], src, ACT.Copy, scale=tg[0:SC, 0:1]).then_inc(vb_ready, 1)

            def gelu(i):
                act.wait_ge(hsum_ready, i + 1)
                nc.scalar.activation(hid[:, :], hsum[:, :], ACT.Gelu).then_inc(hid_ready, 1)

            def split_high(c):
                act.wait_ge(pair_in[c], 16)
                src = wstage[:, c % STAGES]
                dst = (w1_hi, w2_hi)[c // PAIRS][:, :, pair_cols(c)]
                gate = 1.0 if c < PAIRS else tg[:, 1:2]
                nc.scalar.activation(dst, src, ACT.Copy, scale=gate).then_inc(w_hi_ready, 1)

            def step(i, norm, attend, first, second):
                n, o = i + 1, i - 1

                def between(values=(), before=(), before2=()):
                    if type(i) is int and i == -1:
                        for b in values:
                            gate_values(b)
                        for c in before:
                            split_high(c)
                    if type(i) is int and i == 0:
                        for c in before2:
                            split_high(c)

                between(before2=(6,))
                if second:
                    act.wait_ge(ht_done, o + 1)
                    nc.scalar.activation(h_hi[:, :, :], hturn_ps[:, 0:D].rearrange("p (k t) -> p k t", k=KD),
                                         ACT.Copy).then_inc(hhi_ready, 1)
                if attend:
                    act.wait_ge(t1_done, n + 1)
                    nc.scalar.activation(xn1_t[:, :, :], turn_ps[:, 0:D].rearrange("p (k t) -> p k t", k=KD),
                                         ACT.Copy).then_inc(xn1t_ready, 1)
                between(values=(0,), before2=(7,))
                if second:
                    act.wait_ge(c3t_done, o + 1)
                    nc.scalar.activation(c3_t[:, :], bias_ps[0:3 * Q, 0:P], ACT.Copy).then_inc(c3t_ready, 1)
                if attend:
                    act.wait_ge(scores_ready, 2 * n + 2)
                    nc.scalar.activation(probs[:, :], scores[:, :], ACT.Exp, bias=neg_max[:, 0:1],
                                         accum_out=row_sum[:, 0:1]).then_inc(probs_ready, 1)
                    act.wait_ge(pt_done, n + 1)
                    nc.scalar.activation(probs_t[:, :], turn_ps[0:SC, 0:P], ACT.Copy).then_inc(probst_ready, 1)
                between(values=range(1, B), before=(2, 3), before2=(8, 9, 10, 11))
                if type(i) is int and i == -1:
                    act.wait_ge(pu_done, 1)
                    nc.scalar.activation(pu[:, :, :], bias_ps[:, 0:KD * R * L].rearrange("p (k n) -> p k n", k=KD),
                                         ACT.Copy).then_inc(pu_ready, 1)
                    act.wait_ge(b2_in, 48)
                    act.wait_ge(fills_ready, 7)
                    for part, dst in enumerate((b2g, b2g_tmp, b2g)):
                        rows = slice(part * Q, part * Q + L)
                        nc.scalar.activation(dst[rows, :], b2b[rows, :], ACT.Copy,
                                             scale=tg[rows, 1:2]).then_inc(b2g_ready, 1)
                if first:
                    act.wait_ge(comb_ready, i + 1)
                    nc.scalar.activation(c3_parts[:, 0:2, 0:L], comb[:, 2:3, :].to_broadcast([P, 2, L]),
                                         ACT.Copy).then_inc(c3hi_ready, 1)
                alone = type(i) is int and i == 0
                if first and not alone:
                    gelu(i)
                if attend:
                    act.wait_ge(t2_done, n + 1)
                    nc.scalar.activation(x2_t[:, :, :], turn_ps[:, 0:D].rearrange("p (k t) -> p k t", k=KD),
                                         ACT.Copy).then_inc(x2t_ready, 1)
                    nc.scalar.activation(x2_hi[:, :, :], turn_ps[:, 0:D].rearrange("p (k t) -> p k t", k=KD),
                                         ACT.Copy).then_inc(x2hi_ready, 1)
                    between(before=(4, 5))
                    act.wait_ge(zs_ready, n + 1)
                    nc.scalar.activation(ez[:, :, :], zs[:, :, :], ACT.Exp).then_inc(ez_ready, 1)
                if first and alone:
                    gelu(i)

            act.wait_ge(kt_done, 1)
            for m in range(KD):
                nc.scalar.activation(kt[:, m, :], ring[:, m, 0:B * SC], ACT.Copy).then_inc(kt_ready, 1)
            act.wait_ge(gates_in, 32)
            nc.scalar.activation(tg[:, :], gates[:, :], ACT.Tanh).then_inc(tg_ready, 1)
            act.wait_ge(tg_ready, 1)
            split_high(0)
            act.wait_ge(qk_done, 1)
            for m in range(KD):
                src = (att_ps, hturn_ps)[m][:, 0:B * SC]
                nc.scalar.activation(qk[:, m, :], src, ACT.Copy, scale=SCALE).then_inc(qk_ready, 1)
            split_high(1)
            step(*BEFORE[0])
            step(*BEFORE[1])
            step(*BEFORE[2])
            step(*BEFORE[3])
            with act.Fori(*LOOP) as i:
                step(i, True, True, True, True)
            for args in AFTER:
                step(*args)

        @block.vector
        def _(dve):
            def split_low(*pairs):
                for c in pairs:
                    dve.wait_ge(w_hi_ready, c + 1)
                    hi = (w1_hi, w2_hi)[c // PAIRS][:, :, pair_cols(c)].bitcast(F32)
                    lo = (w1_lo, w2_lo)[c // PAIRS][:, :, pair_cols(c)]
                    src = wstage[:, c % STAGES]
                    if c < PAIRS:
                        nc.vector.tensor_tensor(lo, src, hi, ALU.subtract).then_inc(w_lo_ready, 1)
                    else:
                        nc.vector.scalar_tensor_tensor(lo, src, tg[:, 1:2], hi, ALU.mult,
                                                       ALU.subtract).then_inc(w_lo_ready, 1)

            def combine1(i, pair, halves=(0, 1)):
                if 0 in halves:
                    dve.wait_ge(m1_done, PAIRS * i + pair + 1)
                for e in (2 * pair + h for h in halves):
                    half = e % 2
                    product = ring[:, pair % RING, half * D:(half + 1) * D]
                    weight = comb[:, 0, e:e + 1]
                    if pair == 0:
                        ins = nc.vector.tensor_scalar(acc1[:, half, :], product, weight, None, ALU.mult)
                    else:
                        dve.wait_ge(c1_done, L * i + e - 1)
                        ins = nc.vector.scalar_tensor_tensor(acc1[:, half, :], product, weight, acc1[:, half, :],
                                                             ALU.mult, ALU.add)
                    ins.then_inc(c1_done, 1)

            def combine2(o, pair, halves=(0, 1)):
                if 0 in halves:
                    dve.wait_ge(m2_done, PAIRS * o + pair + 1)
                for e in (2 * pair + h for h in halves):
                    half = e % 2
                    product = ring[:, (PAIRS + pair) % RING, half * D:(half + 1) * D]
                    weight = comb_old[:, e:e + 1]
                    if e == 1:
                        ins = nc.vector.tensor_scalar(acc2[:, half, :], product, weight, None, ALU.mult)
                    else:
                        if e == 0:
                            dve.wait_ge(start2_ready, o + 1)
                        else:
                            dve.wait_ge(c2_done, L * o + e - 1)
                        ins = nc.vector.scalar_tensor_tensor(acc2[:, half, :], product, weight, acc2[:, half, :],
                                                             ALU.mult, ALU.add)
                    ins.then_inc(c2_done, 1)

            def xtile(t):
                return xb[:, bass.ds(t, 1), :].rearrange("p a d -> p (a d)")

            def step(i, norm, attend, first, second):
                m, n, o = i + 2, i + 1, i - 1

                alone = type(i) is int and i == 0

                def one(pair, *halves):
                    if alone:
                        if pair in SPREAD:
                            combine1(i, SPREAD[pair], *halves)
                    elif first:
                        combine1(i, pair, *halves)

                def two(pair, *halves):
                    if alone:
                        one(PAIRS + pair, *halves)
                    elif second:
                        combine2(o, pair, *halves)

                def sum1():
                    dve.wait_ge(c1_done, L * (i + 1))
                    nc.vector.tensor_tensor(hsum[:, :], acc1[:, 0, :], acc1[:, 1, :],
                                            ALU.add).then_inc(hsum_ready, 1)

                def between(before=(), before2=()):
                    if type(i) is int and i == -1:
                        split_low(*before)
                    if type(i) is int and i == 0:
                        split_low(*before2)

                if first:
                    dve.wait_ge(comb_ready, i + 1)
                one(0)
                if second:
                    dve.wait_ge(hhi_ready, o + 1)
                    nc.vector.tensor_tensor(h_lo[:, :, :], hturn_ps[:, 0:D].rearrange("p (k t) -> p k t", k=KD),
                                            h_hi[:, :, :].bitcast(F32), ALU.subtract).then_inc(hlo_ready, 1)
                one(1)
                if attend:
                    dve.wait_ge(scores_done, n + 1)
                    nc.vector.tensor_tensor(scores[:, :], att_ps[:, 0:SC],
                                            maskb[:, bass.ds(n, 1), :].rearrange("p a s -> p (a s)"),
                                            ALU.add).then_inc(scores_ready, 1)
                    dve.wait_ge(scores_ready, 2 * n + 1)
                    nc.vector.tensor_reduce(neg_max[:, 0:1], scores[:, :], AX.X, ALU.max,
                                            negate=True).then_inc(scores_ready, 1)
                one(2)
                between(before=(1,), before2=(6,))
                if norm:
                    nc.vector.bn_stats(stats1[:, :], xtile(m)).then_inc(parts1_ready, 1)
                    dve.wait_ge(parts1_ready, m + 1)
                one(3, (0,))
                if norm:
                    nc.vector.bn_aggr(mv1[:, :], stats1[:, :]).then_inc(stats1_ready, 1)
                one(3, (1,))
                if attend:
                    dve.wait_ge(probs_ready, n + 1)
                    nc.vector.reciprocal(inv_sum[:, 0:1], row_sum[:, 0:1]).then_inc(inv_ready, 1)
                between(before2=(7,))
                if second:
                    if not first:
                        dve.wait_ge(out_ready, o)
                    dve.wait_ge(bias_done, o + 1)
                    nc.vector.tensor_tensor(acc2[:, 0, :], bias_ps[:, D:2 * D], xtile(o),
                                            ALU.add).then_inc(start2_ready, 1)
                one(4)
                if attend:
                    dve.wait_ge(inv_ready, n + 1)
                    dve.wait_ge(pv_done, n + 1)
                    nc.vector.scalar_tensor_tensor(xtile(n), att_ps[:, D:2 * D], inv_sum[:, 0:1], xtile(n),
                                                   ALU.mult, ALU.add).then_inc(x1_ready, 1)
                if norm:
                    dve.wait_ge(rstd1_ready, 2 * m + 2)
                    nc.vector.tensor_scalar(xn1[:, :], xtile(m), mv1[:, 0:1], rstd1[:, 0:1], ALU.subtract,
                                            ALU.mult).then_inc(xn1_ready, 1)
                if attend:
                    dve.wait_ge(x1_ready, n + 1)
                if first:
                    dve.wait_ge(c3hi_ready, i + 1)
                    nc.vector.tensor_tensor(c3_parts[:, 2, 0:L], comb[:, 2, :], c3_parts[:, 0, 0:L].bitcast(F32),
                                            ALU.subtract).then_inc(c3lo_ready, 1)
                if attend:
                    nc.vector.bn_stats(stats2[:, :], xtile(n)).then_inc(parts2_ready, 1)
                    dve.wait_ge(parts2_ready, n + 1)
                one(5, (0,))
                if attend:
                    nc.vector.bn_aggr(mv2[:, :], stats2[:, :]).then_inc(stats2_ready, 1)
                one(5, (1,))
                if first and not alone:
                    sum1()
                if attend:
                    dve.wait_ge(rstd2_ready, 2 * n + 2)
                    nc.vector.tensor_scalar(xn2[:, :], xtile(n), mv2[:, 0:1], rstd2[:, 0:1], ALU.subtract,
                                            ALU.mult).then_inc(xn2_ready, 1)
                two(0)
                between(before=(2,), before2=(8,))
                two(1)
                if attend:
                    dve.wait_ge(x2hi_ready, n + 1)
                    nc.vector.tensor_tensor(x2_lo[:, :, :], turn_ps[:, 0:D].rearrange("p (k t) -> p k t", k=KD),
                                            x2_hi[:, :, :].bitcast(F32), ALU.subtract).then_inc(x2lo_ready, 1)
                between(before=(3,), before2=(9,))
                if type(i) is int and i == -1:
                    dve.wait_ge(b2g_ready, 3)
                    nc.vector.scalar_tensor_tensor(b2g[Q:Q + L, :], b2b[Q:Q + L, :], tg[Q:Q + L, 1:2],
                                                   b2g_tmp[Q:Q + L, :].bitcast(F32), ALU.mult,
                                                   ALU.subtract).then_inc(b2glo_ready, 1)
                if alone:
                    sum1()
                two(2)
                two(3, (0,))
                between(before=(4,), before2=(10,))
                if attend:
                    dve.wait_ge(z_done, n + 1)
                    nc.vector.tensor_copy(z[:, :, 0:L], att_ps[:, 128:128 + R * L].rearrange("p (r e) -> p r e", r=R)
                                          ).then_inc(z_read, 1)
                two(3, (1,))
                if attend:
                    dve.wait_ge(fills_ready, 5)
                    dve.wait_ge(z_read, n + 1)
                    for r in range(R):
                        nc.vector.max(top[:, r, :], z[:, r, 0:L]).then_inc(top_ready, 1)
                two(4, (0,))
                between(before=(5,), before2=(11,))
                if attend:
                    dve.wait_ge(top_ready, R * (n + 1))
                    nc.vector.tensor_tensor(zs[:, :, :], z[:, :, 0:L], top[:, :, 0:1].to_broadcast([P, R, L]),
                                            ALU.subtract).then_inc(zs_ready, 1)
                    nc.vector.tensor_copy(wanted[:, :, 0:TOPK], top[:, :, 0:TOPK]).then_inc(wanted_ready, 1)
                two(4, (1,))
                if attend:
                    dve.wait_ge(fills_ready, 5)
                    dve.wait_ge(wanted_ready, n + 1)
                    for r in range(R):
                        nc.vector.match_replace(marked[:, r, :], wanted[:, r, :], z[:, r, :],
                                                PICKED).then_inc(marked_ready, 1)
                two(5, (0,))
                if attend:
                    dve.wait_ge(marked_ready, R * (n + 1))
                    dve.wait_ge(ez_ready, n + 1)
                    nc.vector.scalar_tensor_tensor(picked[:, :, :], marked[:, :, 0:L], PICKED, ez[:, :, :],
                                                   ALU.is_equal, ALU.mult).then_inc(weigh_ready, 1)
                two(5, (1,))
                if attend:
                    dve.wait_ge(weigh_ready, 3 * n + 1)
                    nc.vector.tensor_reduce(zsum[:, :], picked[:, :, :], AX.X, ALU.add).then_inc(weigh_ready, 1)
                if second:
                    dve.wait_ge(c2_done, L * (o + 1))
                    if not (type(o) is int and o == 0):
                        dve.wait_ge(out_stored, 16 * o)
                    nc.vector.tensor_tensor(outb[:, 0, :], acc2[:, 0, :], acc2[:, 1, :],
                                            ALU.add).then_inc(out_ready, 1)
                if first:
                    nc.vector.tensor_copy(comb_old[:, :], comb[:, 1, :]).then_inc(comb_old_ready, 1)
                if attend:
                    dve.wait_ge(weigh_ready, 3 * n + 2)
                    nc.vector.reciprocal(zinv[:, :], zsum[:, :]).then_inc(weigh_ready, 1)
                if attend:
                    dve.wait_ge(weigh_ready, 3 * n + 3)
                    nc.vector.tensor_tensor(comb[:, :, :], picked[:, :, :],
                                            zinv[:, :].rearrange("p (r a) -> p r a", a=1).to_broadcast([P, R, L]),
                                            ALU.mult).then_inc(comb_ready, 1)

            dve.wait_ge(x_first, 16)
            step(*BEFORE[0])
            split_low(0)
            dve.wait_ge(mask_first, 16)
            dve.wait_ge(fills_ready, 5)
            step(*BEFORE[1])
            dve.wait_ge(x_second, 16)
            step(*BEFORE[2])
            dve.wait_ge(mask_rest, 16)
            dve.wait_ge(x_rest, 64)
            step(*BEFORE[3])
            with dve.Fori(*LOOP) as i:
                step(i, True, True, True, True)
            for args in AFTER:
                step(*args)

        @block.tensor
        def _(pe):
            def values(*batches):
                for b in batches:
                    for k in range(KD):
                        mm = nc.tensor.matmul(ring[0:SC, b, 0:D],
                                              ctxb[:, k, b * SC:(b + 1) * SC], wvb[:, k, :],
                                              start=k == 0, stop=k == KD - 1)
                    mm.then_inc(v_done, 1)

            def turn(dst, src):
                return nc.tensor.transpose(dst, src, ident[0:src.shape[0], 0:src.shape[0]])

            def three_passes(dst, a_hi, a_lo, w_hi, w_lo, cols):
                for k in range(KD):
                    nc.tensor.matmul(dst, a_hi[:, k, :], w_hi[:, k, cols], start=k == 0, stop=False)
                    nc.tensor.matmul(dst, a_hi[:, k, :], w_lo[:, k, cols], start=False, stop=False)
                    mm = nc.tensor.matmul(dst, a_lo[:, k, :], w_hi[:, k, cols], start=False, stop=k == KD - 1)
                return mm

            def mixture1(i, pair, beside_second, settle):
                if pair >= RING:
                    pe.wait_ge(c1_done, L * i + 2 * (pair - RING) + 2)
                elif beside_second:
                    pe.wait_ge(c2_done, L * (i - 2) + 2 * (pair + 2) + 2)
                elif settle:
                    pe.wait_ge(c1_done, L * i)
                three_passes(ring[:, pair % RING, :], x2_hi, x2_lo, w1_hi, w1_lo,
                             slice(2 * pair * D, 2 * (pair + 1) * D)).then_inc(m1_done, 1)

            def mixture2(o, pair, beside_first):
                if pair >= RING:
                    pe.wait_ge(c2_done, L * o + 2 * (pair - RING) + 2)
                elif beside_first:
                    pe.wait_ge(c1_done, L * (o + 1) + 2 * (pair + 2) + 2)
                else:
                    pe.wait_ge(c2_done, L * o)
                three_passes(ring[:, (PAIRS + pair) % RING, :], h_hi, h_lo, w2_hi, w2_lo,
                             slice(2 * pair * D, 2 * (pair + 1) * D)).then_inc(m2_done, 1)

            def step(i, norm, attend, first, second):
                n, o = i + 1, i - 1
                after_first = not (type(i) is int and i < 2)

                def m1(pair):
                    if type(i) is int and i == 0:
                        if pair not in SPREAD:
                            return
                        pair = SPREAD[pair]
                        pe.wait_ge(w_lo_ready, pair + 1)
                    if first:
                        mixture1(i, pair, after_first, type(i) is int and i == 1)

                def m2(pair):
                    if type(i) is int and i == 0:
                        m1(PAIRS + pair)
                    if type(i) is int and i == 1:
                        pe.wait_ge(w_lo_ready, PAIRS + pair + 1)
                    if second:
                        mixture2(o, pair, first)

                if first:
                    pe.wait_ge(x2lo_ready, i + 1)
                m1(0)
                if second:
                    pe.wait_ge(hid_ready, o + 1)
                    for k in range(KD):
                        mm = turn(hturn_ps[:, k * P:(k + 1) * P], hid[:, k * P:(k + 1) * P])
                    mm.then_inc(ht_done, 1)
                if attend:
                    pe.wait_ge(xn1_ready, n + 1)
                    for k in range(KD):
                        mm = turn(turn_ps[:, k * P:(k + 1) * P], xn1[:, k * P:(k + 1) * P])
                    mm.then_inc(t1_done, 1)
                if second:
                    pe.wait_ge(c3lo_ready, o + 1)
                    turn(bias_ps[0:3 * Q, 0:P], c3_parts[:, :, :].rearrange("p n q -> p (n q)").bitcast(F32)
                         ).then_inc(c3t_done, 1)
                m1(1)
                if attend:
                    pe.wait_ge(xn1t_ready, n + 1)
                    if not (type(n) is int and n == 0):
                        pe.wait_ge(z_read, n)
                    for k in range(KD):
                        mm = nc.tensor.matmul(att_ps[:, 0:SC], xn1_t[:, k, :],
                                              qk[:, k, bass.ds((n // TPB) * SC, SC)],
                                              start=k == 0, stop=k == KD - 1)
                    mm.then_inc(scores_done, 1)
                if type(i) is int and i == -1:
                    pe.wait_ge(wv_in, 16)
                    values(0)
                m1(2)
                m1(3)
                if attend:
                    pe.wait_ge(probs_ready, n + 1)
                    turn(turn_ps[0:SC, 0:P], probs[:, :]).then_inc(pt_done, 1)
                if second:
                    pe.wait_ge(c3t_ready, o + 1)
                    nc.tensor.matmul(bias_ps[:, D:2 * D], c3_t[:, :], b2g[:, :], start=True,
                                     stop=True).then_inc(bias_done, 1)
                m1(4)
                if attend:
                    if type(i) is int and i < 3:
                        pe.wait_ge(vb_ready, 1 if i < 0 else B)
                    pe.wait_ge(probst_ready, n + 1)
                    nc.tensor.matmul(att_ps[:, D:2 * D], probs_t[:, :],
                                     vb[:, bass.ds(n // TPB, 1), :].rearrange("s a d -> s (a d)"),
                                     start=True, stop=True).then_inc(pv_done, 1)
                if type(i) is int and i == -1:
                    values(*range(1, B))
                    pe.wait_ge(route_in, 32)
                    for m in range(KD):
                        mm = nc.tensor.matmul(bias_ps[:, m * R * L:(m + 1) * R * L], pwb[:, m * P:(m + 1) * P],
                                              utb[:, :], start=True, stop=True)
                    mm.then_inc(pu_done, 1)
                m1(5)
                if second:
                    pe.wait_ge(hlo_ready, o + 1)
                m2(0)
                m2(1)
                if attend:
                    pe.wait_ge(xn2_ready, n + 1)
                    for k in range(KD):
                        mm = turn(turn_ps[:, k * P:(k + 1) * P], xn2[:, k * P:(k + 1) * P])
                    mm.then_inc(t2_done, 1)
                m2(2)
                m2(3)
                if attend:
                    if type(i) is int and i == -1:
                        pe.wait_ge(pu_ready, 1)
                    pe.wait_ge(x2t_ready, n + 1)
                    for k in range(KD):
                        mm = nc.tensor.matmul(att_ps[:, 128:128 + R * L], x2_t[:, k, :], pu[:, k, :],
                                              start=k == 0, stop=k == KD - 1)
                    mm.then_inc(z_done, 1)
                m2(4)
                m2(5)

            pe.wait_ge(wk_in, 32)
            for m in range(KD):
                for k in range(KD):
                    mm = nc.tensor.matmul(ring[:, m, 0:B * SC], wkb[:, k, m * P:(m + 1) * P], ctxb[:, k, :],
                                          start=k == 0, stop=k == KD - 1)
            mm.then_inc(kt_done, 1)
            pe.wait_ge(wq_in, 16)
            pe.wait_ge(kt_ready, KD)
            for m in range(KD):
                for k in range(KD):
                    mm = nc.tensor.matmul((att_ps, hturn_ps)[m][:, 0:B * SC], wqb[:, k, m * P:(m + 1) * P],
                                          kt[:, k, :], start=k == 0, stop=k == KD - 1)
            mm.then_inc(qk_done, 1)
            pe.wait_ge(ident_ready, 1)
            pe.wait_ge(qk_ready, KD)
            step(*BEFORE[1])
            pe.wait_ge(b2glo_ready, 1)
            pe.wait_ge(vb_ready, B)
            step(*BEFORE[2])
            step(*BEFORE[3])
            with pe.Fori(*LOOP) as i:
                step(i, True, True, True, True)
            for args in AFTER:
                step(*args)


def kernel(**inputs):
    import numpy as np
    import concourse.bacc as bacc
    from concourse.bass_utils import run_bass_kernel_spmd

    def turned(a):
        return np.ascontiguousarray(np.asarray(a).T)

    def by_partition(a):
        a = np.asarray(a)
        return np.ascontiguousarray(a.reshape(-1, 128, a.shape[-1]).transpose(1, 0, 2))

    ctx = np.asarray(inputs["ctx_1024"])
    w1, w2 = np.asarray(inputs["L0_ffn_W1"]), np.asarray(inputs["L0_ffn_W2"])
    u = np.concatenate([np.asarray(inputs[f"L0_ffn_U{n}"]) for n in (1, 2, 3)], axis=0)
    arrays = {
        "x": np.ascontiguousarray(inputs["x"]),
        "ctx_t": turned(ctx.reshape(-1, ctx.shape[2])),
        "mask": by_partition(inputs["mask_BxSxS2_ff0"]),
        "g_xattn": np.ascontiguousarray(inputs["g_xattn"]),
        "g_ffn": np.ascontiguousarray(inputs["g_ffn"]),
        "wq": np.ascontiguousarray(inputs["L0_xattn_Wq"]),
        "wk_t": turned(inputs["L0_xattn_Wk"]),
        "wv_t": turned(inputs["L0_xattn_Wv"]),
        "p_w": np.ascontiguousarray(inputs["L0_ffn_P_w"]),
        "u_t": turned(u),
        "w1_t": turned(w1.reshape(-1, w1.shape[2])),
        "w2_t": turned(w2.reshape(-1, w2.shape[2])),
        "b2": np.ascontiguousarray(inputs["L0_ffn_b2"]),
    }
    nc = bacc.Bacc("TRN2", target_bir_lowering=False, num_devices=1)
    feeds, args = {}, []
    for name, a in arrays.items():
        feeds[f"in_{name}"] = a
        args.append(nc.dram_tensor(f"in_{name}", a.shape, mybir.dt.from_np(a.dtype), kind="ExternalInput").ap())
    out = nc.dram_tensor("out", arrays["x"].shape, F32, kind="ExternalOutput").ap()
    gated_xattn_and_routed_ffn(nc, *args, out)
    result = run_bass_kernel_spmd(nc, [feeds], core_ids=[0])
    return result.results[0]["out"]
```

```python
from contextlib import ExitStack

import concourse.bass as bass
from concourse import mybir

F32 = mybir.dt.float32
F32R = mybir.dt.float32r
ALU = mybir.AluOpType
ACT = mybir.ActivationFunctionType
AX = mybir.AxisListType

LN_EPS = 1e-5
LOWEST = -3.4028234663852886e38
PICKED = 3.4028234663852886e38


def gated_xattn_and_routed_ffn(nc, x, x_turned, ctx_t, mask_t, g_xattn, g_ffn, wq, wk_t, wv_t, p_w, u_t, w1_t, w2_t,
                             b2, out):
    P = 128
    B, S, D = x.shape
    SC = mask_t.shape[2]
    L = b2.shape[0]
    KD = D // P
    TILES = B * S // P
    TPB = S // P
    R = 3
    TOPK = 3
    ZW = L + 8 - TOPK
    PAIRS = L // 2
    RING = 4
    STAGES = 6
    Q = 32
    ADDR = p_w.shape[0]
    SCALE = 1.0 / float(D) ** 0.5
    BN = nc.vector.BN_STATS_DIM
    assert D == KD * P == 256 and L % 2 == 0 and 2 * D == 512 and S % P == 0

    x_rows = x.rearrange("b (n p) d -> p (b n) d", p=P)
    out_rows = out.rearrange("b (n p) d -> p (b n) d", p=P)

    with ExitStack() as ctx:
        def sb(name, shape, dt=F32):
            return ctx.enter_context(nc.sbuf_tensor(name, shape, dt))

        def ps(name, shape):
            return ctx.enter_context(nc.psum_tensor(name, shape, F32))

        def sem(name):
            return ctx.enter_context(nc.semaphore(name))

        ring = ps("ring", [P, RING, 2 * D])
        turn_ps = ps("turn_ps", [P, 2 * D])
        hturn_ps = ps("hturn_ps", [P, 2 * D])
        att_ps = ps("att_ps", [P, 2 * D])
        bias_ps = ps("bias_ps", [P, 2 * D])

        xb = sb("xb", [P, TILES, D])
        maskb = sb("maskb", [P, TILES, SC])
        ident = sb("ident", [P, P])
        minus_half = sb("minus_half", [P, 1])
        eps = sb("eps", [P, 1])
        ctxb = sb("ctxb", [P, KD, B * SC])
        wqb = sb("wqb", [P, KD, D])
        wq_stats = sb("wq_stats", [P, KD, BN])
        wq_mv = sb("wq_mv", [P, KD, 2])
        wkb = sb("wkb", [P, KD, D])
        wvb = sb("wvb", [P, KD, D])
        pwb = sb("pwb", [ADDR, D])
        utb = sb("utb", [ADDR, R * L])
        b2b = sb("b2b", [3 * Q, D])
        gates = sb("gates", [P, 2])
        tg = sb("tg", [P, 2])
        b2g = sb("b2g", [3 * Q, D], F32R)
        b2g_tmp = sb("b2g_tmp", [3 * Q, D], F32R)
        kt = sb("kt", [P, KD, B * SC])
        qk = sb("qk", [P, KD, B * SC])
        vb = sb("vb", [SC, B, D])
        pu = sb("pu", [P, KD, R * L])
        wstage = sb("wstage", [P, STAGES, KD, 2 * D])
        w1_hi = sb("w1_hi", [P, KD, L * D], F32R)
        w1_lo = sb("w1_lo", [P, KD, L * D], F32R)
        w2_hi = sb("w2_hi", [P, KD, L * D], F32R) 
        w2_lo = sb("w2_lo", [P, KD, L * D], F32R)

        stats1 = sb("stats1", [P, BN])
        mv1 = sb("mv1", [P, 2])
        var1 = sb("var1", [P, 1])
        rstd1 = sb("rstd1", [P, 1])
        xt = sb("xt", [P, KD, P])
        scores = sb("scores", [P, SC])
        neg_max = sb("neg_max", [P, 1])
        probs = sb("probs", [P, SC])
        row_sum = sb("row_sum", [P, 1])
        inv_sum = sb("inv_sum", [P, 1])
        probs_t = sb("probs_t", [SC, P])
        stats2 = sb("stats2", [P, BN])
        mv2 = sb("mv2", [P, 2])
        var2 = sb("var2", [P, 1])
        rstd2 = sb("rstd2", [P, 1])
        xn2 = sb("xn2", [P, D])
        x2_t = sb("x2_t", [P, KD, P])
        x2_hi = sb("x2_hi", [P, KD, P], F32R)
        x2_lo = sb("x2_lo", [P, KD, P], F32R)
        z = sb("z", [P, R, ZW])
        top = sb("top", [P, R, 8])
        wanted = sb("wanted", [P, R, 8])
        marked = sb("marked", [P, R, ZW])
        zs = sb("zs", [P, R, L])
        ez = sb("ez", [P, R, L])
        picked = sb("picked", [P, R, L])
        zsum = sb("zsum", [P, R])
        zinv = sb("zinv", [P, R])
        comb = sb("comb", [P, R, L])
        comb_old = sb("comb_old", [P, L])
        acc1 = sb("acc1", [P, 2, D])
        hsum = sb("hsum", [P, D])
        hid = sb("hid", [P, D])
        h_hi = sb("h_hi", [P, KD, P], F32R)
        h_lo = sb("h_lo", [P, KD, P], F32R)
        c3_parts = sb("c3_parts", [P, 3, Q], F32R)
        c3_t = sb("c3_t", [3 * Q, P], F32R)
        acc2 = sb("acc2", [P, 2, D])
        outb = sb("outb", [P, 1, D])

        wk_in = sem("wk_in")
        wq_in = sem("wq_in")
        wv_in = sem("wv_in")
        gates_in = sem("gates_in")
        route_in = sem("route_in")
        b2_in = sem("b2_in")
        x_first = sem("x_first")
        x_second = sem("x_second")
        xt_in = sem("xt_in")
        x_rest = sem("x_rest")
        mask_first = sem("mask_first")
        mask_rest = sem("mask_rest")
        pair_in = [sem(f"pair_in{c}") for c in range(2 * PAIRS)]
        ident_ready = sem("ident_ready")
        fills_ready = sem("fills_ready")
        tg_ready = sem("tg_ready")
        kt_done = sem("kt_done")
        qk_done = sem("qk_done")
        v_done = sem("v_done")
        pu_done = sem("pu_done")
        kt_ready = sem("kt_ready")
        centre_ready = sem("centre_ready")
        wq_ready = sem("wq_ready")
        qk_ready = sem("qk_ready")
        vb_ready = sem("vb_ready")
        b2g_ready = sem("b2g_ready")
        pu_ready = sem("pu_ready")
        w_hi_ready = sem("w_hi_ready")
        w_lo_ready = sem("w_lo_ready")
        pool_lo_ready = sem("pool_lo_ready")
        scores_done = sem("scores_done")
        pt_done = sem("pt_done")
        pv_done = sem("pv_done")
        t2_done = sem("t2_done")
        z_done = sem("z_done")
        m1_done = sem("m1_done")
        ht_done = sem("ht_done")
        c3t_done = sem("c3t_done")
        bias_done = sem("bias_done")
        m2_done = sem("m2_done")
        probs_ready = sem("probs_ready")
        probst_ready = sem("probst_ready")
        x2t_ready = sem("x2t_ready")
        x2hi_ready = sem("x2hi_ready")
        ez_ready = sem("ez_ready")
        started1 = sem("started1")
        hid_ready = sem("hid_ready")
        hhi_ready = sem("hhi_ready")
        c3hi_ready = sem("c3hi_ready")
        c3t_ready = sem("c3t_ready")
        parts1_ready = sem("parts1_ready")
        stats1_ready = sem("stats1_ready")
        scores_ready = sem("scores_ready")
        inv_ready = sem("inv_ready")
        x1_ready = sem("x1_ready")
        parts2_ready = sem("parts2_ready")
        stats2_ready = sem("stats2_ready")
        xn2_ready = sem("xn2_ready")
        x2lo_ready = sem("x2lo_ready")
        z_read = sem("z_read")
        top_ready = sem("top_ready")
        zs_ready = sem("zs_ready")
        wanted_ready = sem("wanted_ready")
        marked_ready = sem("marked_ready")
        weigh_ready = sem("weigh_ready")
        comb_ready = sem("comb_ready")
        c1_done = sem("c1_done")
        hsum_ready = sem("hsum_ready")
        hlo_ready = sem("hlo_ready")
        c3lo_ready = sem("c3lo_ready")
        b2glo_ready = sem("b2glo_ready")
        start2_ready = sem("start2_ready")
        c2_done = sem("c2_done")
        out_ready = sem("out_ready")
        rstd1_ready = sem("rstd1_ready")
        rstd2_ready = sem("rstd2_ready")
        out_stored = sem("out_stored")

        FIRST, SECOND = 2, 4
        REST = (TILES - SECOND) // 4
        block = ctx.enter_context(nc.Block())

        def pair_cols(c):
            return slice((c % PAIRS) * 2 * D, (c % PAIRS + 1) * 2 * D)

        POOL_PAIRS = (1, 3, 5)

        def low_part(eng, engine, c, ready):
            eng.wait_ge(w_hi_ready, c + 1)
            hi = (w1_hi, w2_hi)[c // PAIRS][:, :, pair_cols(c)].bitcast(F32)
            lo = (w1_lo, w2_lo)[c // PAIRS][:, :, pair_cols(c)]
            engine.tensor_tensor(lo, wstage[:, c % STAGES], hi, ALU.subtract).then_inc(ready, 1)

        BEFORE = [(-2, True, False, False, False), (-1, True, True, False, False),
                  (0, True, True, True, False), (1, True, True, True, True)]
        AFTER = [(TILES - 2, False, True, True, True), (TILES - 1, False, False, True, True),
                 (TILES, False, False, False, True)]
        LOOP = (2, TILES - 2)
        L1 = L - 2
        SPREAD = {0: 0, 1: 1, 3: 2, 5: 3, 6: 4, 7: 5}

        @block.sync
        def _(sp):
            def load_pair(c):
                src = (w1_t, w2_t)[c // PAIRS].rearrange("(k p) n -> p k n", p=P)[:, :, pair_cols(c)]
                if c >= STAGES:
                    sp.wait_ge(w_lo_ready, c - STAGES + 1)
                sp.dma_start(wstage[:, c % STAGES], src).then_inc(pair_in[c], 16)

            def load_turned(t):
                if not (type(t) is int and t == 0):
                    sp.wait_ge(scores_done, t)
                sp.dma_start(xt[:, :, :], x_turned[:, bass.ds(t, 1), :, :].rearrange("p a k t -> p (a k) t")
                             ).then_inc(xt_in, 16)

            sp.dma_start(ctxb[:, :, :], ctx_t.rearrange("(k p) s -> p k s", p=P)).then_inc(wk_in, 16)
            sp.dma_start(wkb[:, :, :], wk_t.rearrange("(k p) h -> p k h", p=P)).then_inc(wk_in, 16)
            sp.dma_start(wqb[:, :, :], wq.rearrange("(k p) h -> p k h", p=P)).then_inc(wq_in, 16)
            sp.dma_start(xb[:, 0:FIRST, :], x_rows[:, 0:FIRST, :]).then_inc(x_first, 16)
            load_turned(0)
            load_pair(0)
            sp.dma_start(maskb[:, 0:FIRST, :], mask_t[:, 0:FIRST, :]).then_inc(mask_first, 16)
            sp.dma_start(wvb[:, :, :], wv_t.rearrange("(k p) h -> p k h", p=P)).then_inc(wv_in, 16)
            for n, gate in enumerate((g_xattn, g_ffn)):
                sp.dma_start(gates[:, n:n + 1], gate.rearrange("(a n) -> a n", a=1).to_broadcast([P, 1])
                             ).then_inc(gates_in, 16)
            load_pair(1)
            sp.dma_start(pwb[:, :], p_w).then_inc(route_in, 16)
            sp.dma_start(utb[:, :], u_t).then_inc(route_in, 16)
            load_pair(2)
            for n in range(3):
                sp.dma_start(b2b[n * Q:n * Q + L, :], b2).then_inc(b2_in, 16)
            for c in range(3, PAIRS):
                load_pair(c)
            sp.dma_start(xb[:, FIRST:SECOND, :], x_rows[:, FIRST:SECOND, :]).then_inc(x_second, 16)
            for c in range(PAIRS, 2 * PAIRS):
                if c == PAIRS + 2:
                    load_turned(1)
                load_pair(c)
            sp.dma_start(maskb[:, FIRST:TILES, :], mask_t[:, FIRST:TILES, :]).then_inc(mask_rest, 16)
            for n in range(4):
                if n == 1:
                    load_turned(2)
                part = slice(SECOND + n * REST, SECOND + (n + 1) * REST)
                sp.dma_start(xb[:, part, :], x_rows[:, part, :]).then_inc(x_rest, 16)

            def store(o):
                sp.wait_ge(out_ready, o + 1)
                sp.dma_start(out_rows[:, bass.ds(o, 1), :], outb[:, :, :]).then_inc(out_stored, 16)

            with sp.Fori(0, TILES - 3) as o:
                load_turned(o + 3)
                store(o)
            for o in range(TILES - 3, TILES):
                store(o)
            sp.wait_ge(out_stored, 16 * TILES)

        @block.gpsimd
        def _(pool):
            nc.gpsimd.memset(minus_half[:, :], -0.5).then_inc(fills_ready, 1)
            nc.gpsimd.memset(eps[:, :], LN_EPS).then_inc(fills_ready, 1)
            nc.gpsimd.memset(z[:, :, :], LOWEST).then_inc(fills_ready, 1)
            nc.gpsimd.memset(wanted[:, :, :], LOWEST).then_inc(fills_ready, 1)
            nc.gpsimd.memset(ident[:, :], 0.0).then_inc(fills_ready, 1)
            nc.gpsimd.memset(c3_parts[:, :, :].bitcast(F32), 0.0).then_inc(fills_ready, 1)
            nc.gpsimd.memset(b2g[:, :].bitcast(F32), 0.0).then_inc(fills_ready, 1)
            pool.wait_ge(fills_ready, 5)
            nc.gpsimd.affine_select(out=ident[:, :], in_=ident[:, :], compare_op=ALU.not_equal, fill=1.0,
                                    base=0, pattern=[[-1, P]], channel_multiplier=1).then_inc(ident_ready, 1)

            def rstd(n, stats_ready, mv, var, rs, ready):
                pool.wait_ge(stats_ready, n + 1)
                nc.gpsimd.tensor_tensor(var[:, :], mv[:, 1:2], eps[:, :], ALU.add).then_inc(ready, 1)
                pool.wait_ge(ready, 2 * n + 1)
                nc.gpsimd.tensor_tensor(rs[:, :], var[:, :], minus_half[:, :], ALU.pow).then_inc(ready, 1)

            def first_norm(m):
                rstd(m, stats1_ready, mv1, var1, rstd1, rstd1_ready)

            def second_norm(n):
                rstd(n, stats2_ready, mv2, var2, rstd2, rstd2_ready)

            first_norm(0)
            first_norm(1)
            second_norm(0)
            for pair in POOL_PAIRS[:2]:
                low_part(pool, nc.gpsimd, PAIRS + pair, pool_lo_ready)
            first_norm(2)
            second_norm(1)
            for pair in POOL_PAIRS[2:]:
                low_part(pool, nc.gpsimd, PAIRS + pair, pool_lo_ready)
            with pool.Fori(2, TILES - 1) as n:
                first_norm(n + 1)
                second_norm(n)
            second_norm(TILES - 1)

        @block.scalar
        def _(act):
            def gate_values(b):
                act.wait_ge(v_done, b + 1)
                src = ring[0:SC, b, 0:D]
                nc.scalar.activation(vb[:, b, :], src, ACT.Copy, scale=tg[0:SC, 0:1]).then_inc(vb_ready, 1)

            def gelu(i):
                act.wait_ge(hsum_ready, i + 1)
                nc.scalar.activation(hid[:, :], hsum[:, :], ACT.Gelu).then_inc(hid_ready, 1)

            def split_high(c):
                act.wait_ge(pair_in[c], 16)
                src = wstage[:, c % STAGES]
                dst = (w1_hi, w2_hi)[c // PAIRS][:, :, pair_cols(c)]
                nc.scalar.activation(dst, src, ACT.Copy).then_inc(w_hi_ready, 1)

            def step(i, norm, attend, first, second):
                n, o = i + 1, i - 1

                def between(values=(), at_minus_1=(), at_0=()):
                    if type(i) is int and i == -1:
                        for b in values:
                            gate_values(b)
                        for c in at_minus_1:
                            split_high(c)
                    if type(i) is int and i == 0:
                        for c in at_0:
                            split_high(c)

                if first:
                    act.wait_ge(comb_ready, i + 1)
                    act.wait_ge(m1_done, PAIRS * i + 1)
                    for e in (0, 1):
                        nc.scalar.activation(acc1[:, e, :], ring[:, 0, e * D:(e + 1) * D], ACT.Copy,
                                             scale=comb[:, 0, e:e + 1]).then_inc(started1, 1)
                if second:
                    act.wait_ge(ht_done, o + 1)
                    nc.scalar.activation(h_hi[:, :, :], hturn_ps[:, 0:D].rearrange("p (k t) -> p k t", k=KD),
                                         ACT.Copy).then_inc(hhi_ready, 1)
                between(values=(0,), at_0=(8,))
                if second:
                    act.wait_ge(c3t_done, o + 1)
                    nc.scalar.activation(c3_t[:, :], bias_ps[0:3 * Q, 0:P], ACT.Copy).then_inc(c3t_ready, 1)
                if attend:
                    act.wait_ge(scores_ready, 2 * n + 2)
                    nc.scalar.activation(probs[:, :], scores[:, :], ACT.Exp, bias=neg_max[:, 0:1],
                                         accum_out=row_sum[:, 0:1]).then_inc(probs_ready, 1)
                    act.wait_ge(pt_done, n + 1)
                    nc.scalar.activation(probs_t[:, :], turn_ps[0:SC, 0:P], ACT.Copy).then_inc(probst_ready, 1)
                between(values=(1, 2), at_minus_1=(3, 4), at_0=(9, 10, 11))
                if type(i) is int and i == -1:
                    gate_values(3)
                    act.wait_ge(pu_done, 1)
                    nc.scalar.activation(pu[:, :, :], bias_ps[:, 0:KD * R * L].rearrange("p (k n) -> p k n", k=KD),
                                         ACT.Copy).then_inc(pu_ready, 1)
                if first:
                    act.wait_ge(comb_ready, i + 1)
                    nc.scalar.activation(c3_parts[:, 0:2, 0:L], comb[:, 2:3, :].to_broadcast([P, 2, L]),
                                         ACT.Copy).then_inc(c3hi_ready, 1)
                alone = type(i) is int and i == 0
                if alone:
                    act.wait_ge(b2_in, 48)
                    act.wait_ge(fills_ready, 7)
                    for part, dst in enumerate((b2g, b2g_tmp, b2g)):
                        rows = slice(part * Q, part * Q + L)
                        nc.scalar.activation(dst[rows, :], b2b[rows, :], ACT.Copy,
                                             scale=tg[rows, 1:2]).then_inc(b2g_ready, 1)
                if first and not alone:
                    gelu(i)
                if attend:
                    act.wait_ge(t2_done, n + 1)
                    nc.scalar.activation(x2_t[:, :, :], turn_ps[:, 0:D].rearrange("p (k t) -> p k t", k=KD),
                                         ACT.Copy).then_inc(x2t_ready, 1)
                    nc.scalar.activation(x2_hi[:, :, :], turn_ps[:, 0:D].rearrange("p (k t) -> p k t", k=KD),
                                         ACT.Copy).then_inc(x2hi_ready, 1)
                    between(at_minus_1=(5, 6))
                if first and alone:
                    gelu(i)
                if attend:
                    act.wait_ge(zs_ready, n + 1)
                    nc.scalar.activation(ez[:, :, :], zs[:, :, :], ACT.Exp).then_inc(ez_ready, 1)
                if type(i) is int and i == -1:
                    split_high(7)

            split_high(0)
            act.wait_ge(kt_done, 1)
            for m in range(KD):
                nc.scalar.activation(kt[:, m, :], ring[:, 2 + m, 0:B * SC], ACT.Copy).then_inc(kt_ready, 1)
            act.wait_ge(gates_in, 32)
            nc.scalar.activation(tg[:, :], gates[:, :], ACT.Tanh).then_inc(tg_ready, 1)
            act.wait_ge(tg_ready, 1)
            split_high(1)
            act.wait_ge(qk_done, 1)
            for m in range(KD):
                src = (att_ps, hturn_ps)[m][:, 0:B * SC]
                nc.scalar.activation(qk[:, m, :], src, ACT.Copy, scale=SCALE).then_inc(qk_ready, 1)
            split_high(2)
            step(*BEFORE[0])
            step(*BEFORE[1])
            step(*BEFORE[2])
            step(*BEFORE[3])
            with act.Fori(*LOOP) as i:
                step(i, True, True, True, True)
            for args in AFTER:
                step(*args)

        @block.vector
        def _(dve):
            def split_low(*pairs):
                for c in pairs:
                    low_part(dve, nc.vector, c, w_lo_ready)

            def combine1(i, pair, halves=(0, 1)):
                if pair == 0:
                    return
                if 0 in halves:
                    dve.wait_ge(m1_done, PAIRS * i + pair + 1)
                for e in (2 * pair + h for h in halves):
                    half = e % 2
                    product = ring[:, pair % RING, half * D:(half + 1) * D]
                    if pair == 1:
                        dve.wait_ge(started1, 2 * i + half + 1)
                    else:
                        dve.wait_ge(c1_done, L1 * i + e - 3)
                    nc.vector.scalar_tensor_tensor(acc1[:, half, :], product, comb[:, 0, e:e + 1], acc1[:, half, :],
                                                   ALU.mult, ALU.add).then_inc(c1_done, 1)

            def combine2(o, pair, halves=(0, 1)):
                if 0 in halves:
                    dve.wait_ge(m2_done, PAIRS * o + pair + 1)
                for e in (2 * pair + h for h in halves):
                    half = e % 2
                    product = ring[:, (PAIRS + pair) % RING, half * D:(half + 1) * D]
                    weight = comb_old[:, e:e + 1]
                    if e == 1:
                        ins = nc.vector.tensor_scalar(acc2[:, half, :], product, weight, None, ALU.mult)
                    else:
                        if e == 0:
                            dve.wait_ge(start2_ready, o + 1)
                        else:
                            dve.wait_ge(c2_done, L * o + e - 1)
                        ins = nc.vector.scalar_tensor_tensor(acc2[:, half, :], product, weight, acc2[:, half, :],
                                                             ALU.mult, ALU.add)
                    ins.then_inc(c2_done, 1)

            def xtile(t):
                return xb[:, bass.ds(t, 1), :].rearrange("p a d -> p (a d)")

            def step(i, norm, attend, first, second):
                m, n, o = i + 2, i + 1, i - 1
                alone = type(i) is int and i == 0

                def one(pair, *halves):
                    if alone:
                        if pair in SPREAD:
                            combine1(i, SPREAD[pair], *halves)
                    elif first:
                        combine1(i, pair, *halves)

                def two(pair, *halves):
                    if alone:
                        one(PAIRS + pair, *halves)
                    elif second:
                        combine2(o, pair, *halves)

                def sum1():
                    dve.wait_ge(c1_done, L1 * (i + 1))
                    nc.vector.tensor_tensor(hsum[:, :], acc1[:, 0, :], acc1[:, 1, :],
                                            ALU.add).then_inc(hsum_ready, 1)

                def between(at_minus_1=(), at_0=()):
                    if type(i) is int and i == -1:
                        split_low(*at_minus_1)
                    if type(i) is int and i == 0:
                        split_low(*at_0)

                if first:
                    dve.wait_ge(comb_ready, i + 1)
                one(0)
                between(at_minus_1=(1,))
                if second:
                    dve.wait_ge(hhi_ready, o + 1)
                    nc.vector.tensor_tensor(h_lo[:, :, :], hturn_ps[:, 0:D].rearrange("p (k t) -> p k t", k=KD),
                                            h_hi[:, :, :].bitcast(F32), ALU.subtract).then_inc(hlo_ready, 1)
                one(1)
                if attend:
                    dve.wait_ge(scores_done, n + 1)
                    dve.wait_ge(rstd1_ready, 2 * n + 2)
                    nc.vector.scalar_tensor_tensor(scores[:, :], att_ps[:, 0:SC], rstd1[:, 0:1],
                                                   maskb[:, bass.ds(n, 1), :].rearrange("p a s -> p (a s)"),
                                                   ALU.mult, ALU.add).then_inc(scores_ready, 1)
                    dve.wait_ge(scores_ready, 2 * n + 1)
                    nc.vector.tensor_reduce(neg_max[:, 0:1], scores[:, :], AX.X, ALU.max,
                                            negate=True).then_inc(scores_ready, 1)
                one(2)
                between(at_minus_1=(2,), at_0=(6, 8))
                if norm:
                    nc.vector.bn_stats(stats1[:, :], xtile(m)).then_inc(parts1_ready, 1)
                    dve.wait_ge(parts1_ready, m + 1)
                one(3, (0,))
                if norm:
                    nc.vector.bn_aggr(mv1[:, :], stats1[:, :]).then_inc(stats1_ready, 1)
                one(3, (1,))
                if type(i) is int and i == 1:
                    split_low(10)
                if attend:
                    dve.wait_ge(probs_ready, n + 1)
                    nc.vector.reciprocal(inv_sum[:, 0:1], row_sum[:, 0:1]).then_inc(inv_ready, 1)
                one(4)
                if attend:
                    dve.wait_ge(inv_ready, n + 1)
                    dve.wait_ge(pv_done, n + 1)
                    nc.vector.scalar_tensor_tensor(xtile(n), att_ps[:, D:2 * D], inv_sum[:, 0:1], xtile(n),
                                                   ALU.mult, ALU.add).then_inc(x1_ready, 1)
                if attend:
                    dve.wait_ge(x1_ready, n + 1)
                if first:
                    dve.wait_ge(c3hi_ready, i + 1)
                    nc.vector.tensor_tensor(c3_parts[:, 2, 0:L], comb[:, 2, :], c3_parts[:, 0, 0:L].bitcast(F32),
                                            ALU.subtract).then_inc(c3lo_ready, 1)
                if attend:
                    nc.vector.bn_stats(stats2[:, :], xtile(n)).then_inc(parts2_ready, 1)
                    dve.wait_ge(parts2_ready, n + 1)
                if second:
                    if not first:
                        dve.wait_ge(out_ready, o)
                    dve.wait_ge(bias_done, o + 1)
                    nc.vector.tensor_tensor(acc2[:, 0, :], bias_ps[:, D:2 * D], xtile(o),
                                            ALU.add).then_inc(start2_ready, 1)
                if attend:
                    nc.vector.bn_aggr(mv2[:, :], stats2[:, :]).then_inc(stats2_ready, 1)
                one(5)
                if alone:
                    dve.wait_ge(b2g_ready, 3)
                    nc.vector.scalar_tensor_tensor(b2g[Q:Q + L, :], b2b[Q:Q + L, :], tg[Q:Q + L, 1:2],
                                                   b2g_tmp[Q:Q + L, :].bitcast(F32), ALU.mult,
                                                   ALU.subtract).then_inc(b2glo_ready, 1)
                between(at_minus_1=(3,))
                if attend:
                    dve.wait_ge(rstd2_ready, 2 * n + 2)
                    nc.vector.tensor_scalar(xn2[:, :], xtile(n), mv2[:, 0:1], rstd2[:, 0:1], ALU.subtract,
                                            ALU.mult).then_inc(xn2_ready, 1)
                if first and not alone:
                    sum1()
                two(0)
                between(at_minus_1=(4,))
                two(1)
                if attend:
                    dve.wait_ge(x2hi_ready, n + 1)
                    nc.vector.tensor_tensor(x2_lo[:, :, :], turn_ps[:, 0:D].rearrange("p (k t) -> p k t", k=KD),
                                            x2_hi[:, :, :].bitcast(F32), ALU.subtract).then_inc(x2lo_ready, 1)
                between(at_minus_1=(5,))
                if alone:
                    sum1()
                two(2)
                two(3, (0,))
                if attend:
                    dve.wait_ge(z_done, n + 1)
                    nc.vector.tensor_copy(z[:, :, 0:L], att_ps[:, 128:128 + R * L].rearrange("p (r e) -> p r e", r=R)
                                          ).then_inc(z_read, 1)
                two(3, (1,))
                if attend:
                    dve.wait_ge(fills_ready, 5)
                    dve.wait_ge(z_read, n + 1)
                    for r in range(R):
                        nc.vector.max(top[:, r, :], z[:, r, 0:L]).then_inc(top_ready, 1)
                two(4, (0,))
                if attend:
                    dve.wait_ge(top_ready, R * (n + 1))
                    nc.vector.tensor_tensor(zs[:, :, :], z[:, :, 0:L], top[:, :, 0:1].to_broadcast([P, R, L]),
                                            ALU.subtract).then_inc(zs_ready, 1)
                    nc.vector.tensor_copy(wanted[:, :, 0:TOPK], top[:, :, 0:TOPK]).then_inc(wanted_ready, 1)
                two(4, (1,))
                if attend:
                    dve.wait_ge(fills_ready, 5)
                    dve.wait_ge(wanted_ready, n + 1)
                    for r in range(R):
                        nc.vector.match_replace(marked[:, r, :], wanted[:, r, :], z[:, r, :],
                                                PICKED).then_inc(marked_ready, 1)
                two(5, (0,))
                if attend:
                    dve.wait_ge(marked_ready, R * (n + 1))
                    dve.wait_ge(ez_ready, n + 1)
                    nc.vector.scalar_tensor_tensor(picked[:, :, :], marked[:, :, 0:L], PICKED, ez[:, :, :],
                                                   ALU.is_equal, ALU.mult).then_inc(weigh_ready, 1)
                two(5, (1,))
                if attend:
                    dve.wait_ge(weigh_ready, 3 * n + 1)
                    nc.vector.tensor_reduce(zsum[:, :], picked[:, :, :], AX.X, ALU.add).then_inc(weigh_ready, 1)
                if second:
                    dve.wait_ge(c2_done, L * (o + 1))
                    if not (type(o) is int and o == 0):
                        dve.wait_ge(out_stored, 16 * o)
                    nc.vector.tensor_tensor(outb[:, 0, :], acc2[:, 0, :], acc2[:, 1, :],
                                            ALU.add).then_inc(out_ready, 1)
                if first:
                    nc.vector.tensor_scalar(comb_old[:, :], comb[:, 1, :], tg[:, 1:2], None,
                                            ALU.mult)
                if attend:
                    dve.wait_ge(weigh_ready, 3 * n + 2)
                    nc.vector.reciprocal(zinv[:, :], zsum[:, :]).then_inc(weigh_ready, 1)
                if attend:
                    dve.wait_ge(weigh_ready, 3 * n + 3)
                    nc.vector.tensor_tensor(comb[:, :, :], picked[:, :, :],
                                            zinv[:, :].rearrange("p (r a) -> p r a", a=1).to_broadcast([P, R, L]),
                                            ALU.mult).then_inc(comb_ready, 1)

            dve.wait_ge(wq_in, 16)
            for k in range(KD):
                nc.vector.bn_stats(wq_stats[:, k, :], wqb[:, k, :]).then_inc(centre_ready, 1)
            for k in range(KD):
                dve.wait_ge(centre_ready, k + 1)
                nc.vector.bn_aggr(wq_mv[:, k, :], wq_stats[:, k, :]).then_inc(centre_ready, 1)
            for k in range(KD):
                dve.wait_ge(centre_ready, KD + k + 1)
                nc.vector.tensor_scalar(wqb[:, k, :], wqb[:, k, :], wq_mv[:, k, 0:1], None,
                                        ALU.subtract).then_inc(wq_ready, 1)
            dve.wait_ge(x_first, 16)
            step(*BEFORE[0])
            split_low(0)
            dve.wait_ge(mask_first, 16)
            dve.wait_ge(fills_ready, 5)
            step(*BEFORE[1])
            dve.wait_ge(x_second, 16)
            step(*BEFORE[2])
            dve.wait_ge(mask_rest, 16)
            step(*BEFORE[3])
            dve.wait_ge(x_rest, 64)
            with dve.Fori(*LOOP) as i:
                step(i, True, True, True, True)
            for args in AFTER:
                step(*args)

        @block.tensor
        def _(pe):
            def values(*batches):
                for b in batches:
                    for k in range(KD):
                        mm = nc.tensor.matmul(ring[0:SC, b, 0:D],
                                              ctxb[:, k, b * SC:(b + 1) * SC], wvb[:, k, :],
                                              start=k == 0, stop=k == KD - 1)
                    mm.then_inc(v_done, 1)

            def turn(dst, src):
                return nc.tensor.transpose(dst, src, ident[0:src.shape[0], 0:src.shape[0]])

            def three_passes(dst, a_hi, a_lo, w_hi, w_lo, cols):
                for k in range(KD):
                    nc.tensor.matmul(dst, a_hi[:, k, :], w_hi[:, k, cols], start=k == 0, stop=False)
                    nc.tensor.matmul(dst, a_hi[:, k, :], w_lo[:, k, cols], start=False, stop=False)
                    mm = nc.tensor.matmul(dst, a_lo[:, k, :], w_hi[:, k, cols], start=False, stop=k == KD - 1)
                return mm

            def mixture1(i, pair, beside_second, settle):
                if pair == RING:
                    pe.wait_ge(started1, 2 * i + 2)
                elif pair > RING:
                    pe.wait_ge(c1_done, L1 * i + 2 * (pair - RING))
                elif beside_second:
                    pe.wait_ge(c2_done, L * (i - 2) + 2 * (pair + 2) + 2)
                elif settle:
                    pe.wait_ge(c1_done, L1 * i)
                three_passes(ring[:, pair % RING, :], x2_hi, x2_lo, w1_hi, w1_lo,
                             slice(2 * pair * D, 2 * (pair + 1) * D)).then_inc(m1_done, 1)

            def mixture2(o, pair, beside_first):
                if pair >= RING:
                    pe.wait_ge(c2_done, L * o + 2 * (pair - RING) + 2)
                elif beside_first:
                    pe.wait_ge(c1_done, L1 * (o + 1) + 2 * (pair + 2))
                else:
                    pe.wait_ge(c2_done, L * o)
                three_passes(ring[:, (PAIRS + pair) % RING, :], h_hi, h_lo, w2_hi, w2_lo,
                             slice(2 * pair * D, 2 * (pair + 1) * D)).then_inc(m2_done, 1)

            def step(i, norm, attend, first, second):
                n, o = i + 1, i - 1
                after_first = not (type(i) is int and i < 2)

                def m1(pair):
                    if type(i) is int and i == 0:
                        if pair not in SPREAD:
                            return
                        pair = SPREAD[pair]
                        pe.wait_ge(w_lo_ready, pair + 1)
                    if first:
                        mixture1(i, pair, after_first, type(i) is int and i == 1)

                def m2(pair):
                    if type(i) is int and i == 0:
                        m1(PAIRS + pair)
                    if type(i) is int and i == 1:
                        if pair in POOL_PAIRS:
                            pe.wait_ge(pool_lo_ready, POOL_PAIRS.index(pair) + 1)
                        else:
                            done = sum(p not in POOL_PAIRS for p in range(pair + 1))
                            pe.wait_ge(w_lo_ready, PAIRS + done)
                    if second:
                        mixture2(o, pair, first)

                if first:
                    pe.wait_ge(x2lo_ready, i + 1)
                m1(0)
                if second:
                    pe.wait_ge(hid_ready, o + 1)
                    for k in range(KD):
                        mm = turn(hturn_ps[:, k * P:(k + 1) * P], hid[:, k * P:(k + 1) * P])
                    mm.then_inc(ht_done, 1)
                if second:
                    pe.wait_ge(c3lo_ready, o + 1)
                    turn(bias_ps[0:3 * Q, 0:P], c3_parts[:, :, :].rearrange("p n q -> p (n q)").bitcast(F32)
                         ).then_inc(c3t_done, 1)
                m1(1)
                if attend:
                    pe.wait_ge(xt_in, 16 * (n + 1))
                    if not (type(n) is int and n == 0):
                        pe.wait_ge(z_read, n)
                    for k in range(KD):
                        mm = nc.tensor.matmul(att_ps[:, 0:SC], xt[:, k, :],
                                              qk[:, k, bass.ds((n // TPB) * SC, SC)],
                                              start=k == 0, stop=k == KD - 1)
                    mm.then_inc(scores_done, 1)
                if type(i) is int and i == -1:
                    values(2)
                m1(2)
                m1(3)
                if attend:
                    pe.wait_ge(probs_ready, n + 1)
                    turn(turn_ps[0:SC, 0:P], probs[:, :]).then_inc(pt_done, 1)
                if second:
                    if type(i) is int and i == 1:
                        pe.wait_ge(b2glo_ready, 1)
                    pe.wait_ge(c3t_ready, o + 1)
                    nc.tensor.matmul(bias_ps[:, D:2 * D], c3_t[:, :], b2g[:, :], start=True,
                                     stop=True).then_inc(bias_done, 1)
                m1(4)
                if attend:
                    if type(i) is int and i < 3:
                        pe.wait_ge(vb_ready, 1 if i < 0 else B)
                    pe.wait_ge(probst_ready, n + 1)
                    nc.tensor.matmul(att_ps[:, D:2 * D], probs_t[:, :],
                                     vb[:, bass.ds(n // TPB, 1), :].rearrange("s a d -> s (a d)"),
                                     start=True, stop=True).then_inc(pv_done, 1)
                if type(i) is int and i == -1:
                    values(3)
                    pe.wait_ge(route_in, 32)
                    for m in range(KD):
                        mm = nc.tensor.matmul(bias_ps[:, m * R * L:(m + 1) * R * L], pwb[:, m * P:(m + 1) * P],
                                              utb[:, :], start=True, stop=True)
                    mm.then_inc(pu_done, 1)
                m1(5)
                if second:
                    pe.wait_ge(hlo_ready, o + 1)
                m2(0)
                m2(1)
                if attend:
                    pe.wait_ge(xn2_ready, n + 1)
                    for k in range(KD):
                        mm = turn(turn_ps[:, k * P:(k + 1) * P], xn2[:, k * P:(k + 1) * P])
                    mm.then_inc(t2_done, 1)
                m2(2)
                m2(3)
                if attend:
                    if type(i) is int and i == -1:
                        pe.wait_ge(pu_ready, 1)
                    pe.wait_ge(x2t_ready, n + 1)
                    for k in range(KD):
                        mm = nc.tensor.matmul(att_ps[:, 128:128 + R * L], x2_t[:, k, :], pu[:, k, :],
                                              start=k == 0, stop=k == KD - 1)
                    mm.then_inc(z_done, 1)
                m2(4)
                m2(5)

            pe.wait_ge(wk_in, 32)
            for m in range(KD):
                for k in range(KD):
                    mm = nc.tensor.matmul(ring[:, 2 + m, 0:B * SC], wkb[:, k, m * P:(m + 1) * P], ctxb[:, k, :],
                                          start=k == 0, stop=k == KD - 1)
            mm.then_inc(kt_done, 1)
            pe.wait_ge(wv_in, 16)
            values(0)
            pe.wait_ge(wq_ready, KD)
            pe.wait_ge(kt_ready, KD)
            for m in range(KD):
                for k in range(KD):
                    mm = nc.tensor.matmul((att_ps, hturn_ps)[m][:, 0:B * SC], wqb[:, k, m * P:(m + 1) * P],
                                          kt[:, k, :], start=k == 0, stop=k == KD - 1)
            mm.then_inc(qk_done, 1)
            values(1)
            pe.wait_ge(ident_ready, 1)
            pe.wait_ge(qk_ready, KD)
            step(*BEFORE[1])
            pe.wait_ge(vb_ready, B)
            step(*BEFORE[2])
            step(*BEFORE[3])
            with pe.Fori(*LOOP) as i:
                step(i, True, True, True, True)
            for args in AFTER:
                step(*args)


def kernel(**inputs):
    import numpy as np
    import concourse.bacc as bacc
    from concourse.bass_utils import run_bass_kernel_spmd

    def turned(a):
        return np.ascontiguousarray(np.asarray(a).T)

    def by_partition(a):
        a = np.asarray(a)
        return np.ascontiguousarray(a.reshape(-1, 128, a.shape[-1]).transpose(1, 0, 2))

    ctx = np.asarray(inputs["ctx_1024"])
    w1, w2 = np.asarray(inputs["L0_ffn_W1"]), np.asarray(inputs["L0_ffn_W2"])
    u = np.concatenate([np.asarray(inputs[f"L0_ffn_U{n}"]) for n in (1, 2, 3)], axis=0)
    arrays = {
        "x": np.ascontiguousarray(inputs["x"]),
        "x_turned": np.ascontiguousarray(
            np.asarray(inputs["x"]).reshape(-1, 128, inputs["x"].shape[2] // 128, 128).transpose(3, 0, 2, 1)),
        "ctx_t": turned(ctx.reshape(-1, ctx.shape[2])),
        "mask": by_partition(inputs["mask_BxSxS2_ff0"]),
        "g_xattn": np.ascontiguousarray(inputs["g_xattn"]),
        "g_ffn": np.ascontiguousarray(inputs["g_ffn"]),
        "wq": np.ascontiguousarray(inputs["L0_xattn_Wq"]),
        "wk_t": turned(inputs["L0_xattn_Wk"]),
        "wv_t": turned(inputs["L0_xattn_Wv"]),
        "p_w": np.ascontiguousarray(inputs["L0_ffn_P_w"]),
        "u_t": turned(u),
        "w1_t": turned(w1.reshape(-1, w1.shape[2])),
        "w2_t": turned(w2.reshape(-1, w2.shape[2])),
        "b2": np.ascontiguousarray(inputs["L0_ffn_b2"]),
    }
    nc = bacc.Bacc("TRN2", target_bir_lowering=False, num_devices=1)
    feeds, args = {}, []
    for name, a in arrays.items():
        feeds[f"in_{name}"] = a
        args.append(nc.dram_tensor(f"in_{name}", a.shape, mybir.dt.from_np(a.dtype), kind="ExternalInput").ap())
    out = nc.dram_tensor("out", arrays["x"].shape, F32, kind="ExternalOutput").ap()
    gated_xattn_and_routed_ffn(nc, *args, out)
    result = run_bass_kernel_spmd(nc, [feeds], core_ids=[0])
    return result.results[0]["out"]
```
